# Optimizing a Trainium2 kernel written in Bass

```python
import numpy as np
import jax
import jax.numpy as jnp

def _softmax(x, axis=-1):
    return jax.nn.softmax(x, axis=axis)

def _gelu(x):
    return jax.nn.gelu(x, approximate=True)

def _silu(x):
    return jax.nn.silu(x)

def _sigmoid(x):
    return jax.nn.sigmoid(x)

def _layernorm(x, axis=-1, eps=1e-05):
    m = jnp.mean(x, axis=axis, keepdims=True)
    v = jnp.var(x, axis=axis, keepdims=True)
    return (x - m) / jnp.sqrt(v + eps)

def _scatter_add(tgt, idx, src, axis=0):
    return tgt.at[idx].add(src)

def _segment_sum(src, seg, n):
    return jax.ops.segment_sum(src, seg, n)
kernel_name = 'mk_conv_seq_d2_conv_nchw192_r2_664234'

def setup_inputs(seed: int=0):
    np.random.seed(seed)
    _w = jnp.asarray

    def _rec_inputs():
        import jax
        import jax.numpy as jnp
        _gk = jax.random.key(seed)
        x = -4.65e-05 + 0.9999 * jax.random.normal(jax.random.fold_in(_gk, 1), (4, 96, 128, 128), jnp.float32)
        return x
    x = _rec_inputs()

    def _L0_conv_setup():
        import jax, jax.numpy as jnp
        import numpy as np
        from jax import lax
        DIM, HEADS, WS = (96, 4, 8)
        ADIM = int(DIM * 0.5)
        BDIM = DIM - ADIM
        REDIM = DIM // 4
        SCALE = (ADIM // HEADS) ** (-0.5)
        EPS = 1e-06
        SHIFT = True

        def conv1x1(x, w, b=None):
            y = jnp.einsum('bchw,oc->bohw', x, w)
            return y if b is None else y + b[None, :, None, None]

        def layernorm2d(x, w, b):
            mu = x.mean(1, keepdims=True)
            var = ((x - mu) ** 2).mean(1, keepdims=True)
            y = (x - mu) / jnp.sqrt(var + EPS)
            return w[None, :, None, None] * y + b[None, :, None, None]

        def to_windows(x, heads, ws):
            B, C, H, W = x.shape
            c = C // heads
            x = x.reshape(B, heads, c, H // ws, ws, W // ws, ws)
            x = x.transpose(0, 3, 5, 1, 4, 6, 2)
            return x.reshape(B * (H // ws) * (W // ws), heads, ws * ws, c)

        def from_windows(y, B, H, W, heads, ws):
            c = y.shape[-1]
            y = y.reshape(B, H // ws, W // ws, heads, ws, ws, c)
            y = y.transpose(0, 3, 6, 1, 4, 2, 5)
            return y.reshape(B, heads * c, H, W)
        key = jax.random.key(seed)
        ks = jax.random.split(key, 12)
        s = 0.02
        return {'x0': jax.random.normal(ks[0], (4, DIM, 128, 128), jnp.float32), 'ln_w': jnp.ones((DIM,), jnp.float32), 'ln_b': jnp.zeros((DIM,), jnp.float32), 'qk_w': jax.random.normal(ks[1], (2 * ADIM, DIM), jnp.float32) * s, 'qk_b': jnp.zeros((2 * ADIM,), jnp.float32), 'vs_w': jax.random.normal(ks[2], (DIM, DIM), jnp.float32) * s, 'vs_b': jnp.zeros((DIM,), jnp.float32), 'depth_w': jax.random.normal(ks[3], (DIM, 1, 3, 3), jnp.float32) * s, 'depth_b': jnp.zeros((DIM,), jnp.float32), 'fu1_w': jax.random.normal(ks[4], (REDIM, DIM), jnp.float32) * s, 'fu2_w': jax.random.normal(ks[5], (DIM, REDIM), jnp.float32) * s, 'proj_w': jax.random.normal(ks[6], (DIM, DIM), jnp.float32) * s, 'proj_b': jnp.zeros((DIM,), jnp.float32)}
    _L0_conv_all = _L0_conv_setup()
    _L0_conv_in = {k: v for k, v in _L0_conv_all.items() if k in ('ln_w', 'ln_b', 'qk_w', 'qk_b', 'vs_w', 'vs_b', 'depth_w', 'depth_b', 'fu1_w', 'fu2_w', 'proj_w', 'proj_b')}
    del _L0_conv_all

    def _L1_conv_setup():
        import jax, jax.numpy as jnp
        import numpy as np
        DIM = 96
        K = 3
        RED = 4
        B, H, W = (4, 128, 128)
        EPS = 1e-05

        def _make_mask():
            m = np.ones((DIM, 1, K, K), np.float32)
            m[:, :, K // 2, K // 2:] = 0.0
            m[:, :, K // 2 + 1:] = 0.0
            return jnp.asarray(m)
        MASK = _make_mask()
        key = jax.random.key(seed)
        ks = jax.random.split(key, 4)
        r = DIM // RED
        return {'x': jax.random.normal(ks[0], (B, DIM, H, W), jnp.float32), 'w1': jax.random.normal(ks[1], (r, DIM), jnp.float32) * 0.05, 'gamma': jnp.ones((r,), jnp.float32), 'beta': jnp.zeros((r,), jnp.float32), 'running_mean': jnp.zeros((r,), jnp.float32), 'running_var': jnp.ones((r,), jnp.float32), 'w2': jax.random.normal(ks[2], (DIM * K * K, r), jnp.float32) * 0.05, 'b2': jnp.zeros((DIM * K * K,), jnp.float32), 'bias': jnp.zeros((DIM,), jnp.float32)}
    _L1_conv_all = _L1_conv_setup()
    _L1_conv_in = {k: v for k, v in _L1_conv_all.items() if k in ('w1', 'gamma', 'beta', 'running_mean', 'running_var', 'w2', 'b2', 'bias')}
    del _L1_conv_all
    return {'x': x, 'L0_conv_ln_w': _L0_conv_in['ln_w'], 'L0_conv_ln_b': _L0_conv_in['ln_b'], 'L0_conv_qk_w': _L0_conv_in['qk_w'], 'L0_conv_qk_b': _L0_conv_in['qk_b'], 'L0_conv_vs_w': _L0_conv_in['vs_w'], 'L0_conv_vs_b': _L0_conv_in['vs_b'], 'L0_conv_depth_w': _L0_conv_in['depth_w'], 'L0_conv_depth_b': _L0_conv_in['depth_b'], 'L0_conv_fu1_w': _L0_conv_in['fu1_w'], 'L0_conv_fu2_w': _L0_conv_in['fu2_w'], 'L0_conv_proj_w': _L0_conv_in['proj_w'], 'L0_conv_proj_b': _L0_conv_in['proj_b'], 'L1_conv_w1': _L1_conv_in['w1'], 'L1_conv_gamma': _L1_conv_in['gamma'], 'L1_conv_beta': _L1_conv_in['beta'], 'L1_conv_running_mean': _L1_conv_in['running_mean'], 'L1_conv_running_var': _L1_conv_in['running_var'], 'L1_conv_w2': _L1_conv_in['w2'], 'L1_conv_b2': _L1_conv_in['b2'], 'L1_conv_bias': _L1_conv_in['bias']}

def reference(x, L0_conv_ln_w, L0_conv_ln_b, L0_conv_qk_w, L0_conv_qk_b, L0_conv_vs_w, L0_conv_vs_b, L0_conv_depth_w, L0_conv_depth_b, L0_conv_fu1_w, L0_conv_fu2_w, L0_conv_proj_w, L0_conv_proj_b, L1_conv_w1, L1_conv_gamma, L1_conv_beta, L1_conv_running_mean, L1_conv_running_var, L1_conv_w2, L1_conv_b2, L1_conv_bias):
    import jax
    import jax.numpy as jnp

    def _L0_conv_ref(x0, ln_w, ln_b, qk_w, qk_b, vs_w, vs_b, depth_w, depth_b, fu1_w, fu2_w, proj_w, proj_b):
        import jax, jax.numpy as jnp
        import numpy as np
        from jax import lax
        DIM, HEADS, WS = (96, 4, 8)
        ADIM = int(DIM * 0.5)
        BDIM = DIM - ADIM
        REDIM = DIM // 4
        SCALE = (ADIM // HEADS) ** (-0.5)
        EPS = 1e-06
        SHIFT = True

        def conv1x1(x, w, b=None):
            y = jnp.einsum('bchw,oc->bohw', x, w)
            return y if b is None else y + b[None, :, None, None]

        def layernorm2d(x, w, b):
            mu = x.mean(1, keepdims=True)
            var = ((x - mu) ** 2).mean(1, keepdims=True)
            y = (x - mu) / jnp.sqrt(var + EPS)
            return w[None, :, None, None] * y + b[None, :, None, None]

        def to_windows(x, heads, ws):
            B, C, H, W = x.shape
            c = C // heads
            x = x.reshape(B, heads, c, H // ws, ws, W // ws, ws)
            x = x.transpose(0, 3, 5, 1, 4, 6, 2)
            return x.reshape(B * (H // ws) * (W // ws), heads, ws * ws, c)

        def from_windows(y, B, H, W, heads, ws):
            c = y.shape[-1]
            y = y.reshape(B, H // ws, W // ws, heads, ws, ws, c)
            y = y.transpose(0, 3, 6, 1, 4, 2, 5)
            return y.reshape(B, heads * c, H, W)
        B, C, H, W = x0.shape
        x = layernorm2d(x0, ln_w, ln_b)
        qk = conv1x1(x, qk_w, qk_b)
        q, k = (qk[:, :ADIM], qk[:, ADIM:])
        vs = conv1x1(x, vs_w, vs_b)
        local = lax.conv_general_dilated(vs, depth_w, window_strides=(1, 1), padding='SAME', feature_group_count=C, dimension_numbers=('NCHW', 'OIHW', 'NCHW')) + depth_b[None, :, None, None]
        v1, v2 = (vs[:, :ADIM], vs[:, ADIM:])
        if SHIFT:
            sh = (-WS // 2, -WS // 2)
            q = jnp.roll(q, sh, axis=(2, 3))
            k = jnp.roll(k, sh, axis=(2, 3))
            v1 = jnp.roll(v1, sh, axis=(2, 3))
        qw = to_windows(q, HEADS, WS)
        kw = to_windows(k, HEADS, WS)
        vw = to_windows(v1, HEADS, WS)
        atn = jnp.einsum('nhqc,nhkc->nhqk', qw, kw) * SCALE
        atn = jax.nn.softmax(atn, axis=-1)
        yw = jnp.einsum('nhqk,nhkc->nhqc', atn, vw)
        y = from_windows(yw, B, H, W, HEADS, WS)
        if SHIFT:
            y = jnp.roll(y, (WS // 2, WS // 2), axis=(2, 3))
        y = jnp.concatenate([y, v2], axis=1)
        s = (y + local).mean(axis=(2, 3), keepdims=True)
        ca = jax.nn.sigmoid(conv1x1(jax.nn.leaky_relu(conv1x1(s, fu1_w), 0.2), fu2_w))
        y = y * ca + local * (1.0 - ca)
        y = conv1x1(y, proj_w, proj_b)
        return y + x0

    def _L1_conv_ref(x, w1, gamma, beta, running_mean, running_var, w2, b2, bias):
        import jax, jax.numpy as jnp
        import numpy as np
        DIM = 96
        K = 3
        RED = 4
        B, H, W = (4, 128, 128)
        EPS = 1e-05

        def _make_mask():
            m = np.ones((DIM, 1, K, K), np.float32)
            m[:, :, K // 2, K // 2:] = 0.0
            m[:, :, K // 2 + 1:] = 0.0
            return jnp.asarray(m)
        MASK = _make_mask()
        b, c, h, w = x.shape
        pooled = x.mean(axis=(2, 3))
        t = pooled @ w1.T
        t = gamma * (t - running_mean) * jax.lax.rsqrt(running_var + EPS) + beta
        t = jax.nn.relu(t)
        wt = t @ w2.T + b2
        wt = wt.reshape(b * DIM, 1, K, K) * jnp.tile(MASK, (b, 1, 1, 1))
        out = jax.lax.conv_general_dilated(x.reshape(1, b * c, h, w), wt, window_strides=(1, 1), padding=((1, 1), (1, 1)), feature_group_count=b * DIM, dimension_numbers=('NCHW', 'OIHW', 'NCHW'))
        out = out + jnp.tile(bias, (b,))[None, :, None, None]
        return out.reshape(b, c, h, w)

    def _gn(v, G=32, eps=1e-05):
        B_, C_, H_, W_ = v.shape
        g = v.reshape(B_, G, C_ // G, H_, W_)
        m = jnp.mean(g, axis=(2, 3, 4), keepdims=True)
        s = jnp.var(g, axis=(2, 3, 4), keepdims=True)
        return ((g - m) / jnp.sqrt(s + eps)).reshape(v.shape)

    def _ln_c(v, eps=1e-06):
        m = jnp.mean(v, axis=1, keepdims=True)
        s = jnp.var(v, axis=1, keepdims=True)
        return (v - m) / jnp.sqrt(s + eps)

    def _ln_t(v, eps=1e-05):
        m = jnp.mean(v, axis=-1, keepdims=True)
        s = jnp.var(v, axis=-1, keepdims=True)
        return (v - m) / jnp.sqrt(s + eps)

    def _to_tokens(v):
        B_, C_, H_, W_ = v.shape
        return v.reshape(B_, C_, H_ * W_).transpose(0, 2, 1)

    def _from_tokens(t, like):
        B_, C_, H_, W_ = like.shape
        return t.transpose(0, 2, 1).reshape(B_, C_, H_, W_)
    x = _L0_conv_ref(x, L0_conv_ln_w, L0_conv_ln_b, L0_conv_qk_w, L0_conv_qk_b, L0_conv_vs_w, L0_conv_vs_b, L0_conv_depth_w, L0_conv_depth_b, L0_conv_fu1_w, L0_conv_fu2_w, L0_conv_proj_w, L0_conv_proj_b)
    x = _L1_conv_ref(x, L1_conv_w1, L1_conv_gamma, L1_conv_beta, L1_conv_running_mean, L1_conv_running_var, L1_conv_w2, L1_conv_b2, L1_conv_bias)
    return x

_drawn_inputs = setup_inputs


def setup_inputs(seed=0):
    import zlib

    import numpy as np

    out = dict(_drawn_inputs(seed))
    spreads = {'L0_conv_ln_w': (1.0, 0.6),
     'L0_conv_ln_b': (0.0, 0.8),
     'L0_conv_qk_b': (0.0, 0.8),
     'L0_conv_vs_b': (0.0, 0.77),
     'L0_conv_depth_b': (0.0, 0.535),
     'L0_conv_proj_b': (0.0, 0.1),
     'L1_conv_gamma': (1.0, 0.2),
     'L1_conv_beta': (0.0, 0.1),
     'L1_conv_running_mean': (0.0, 0.1),
     'L1_conv_running_var': (1.0, 0.6),
     'L1_conv_b2': (0.0, 0.1),
     'L1_conv_bias': (0.0, 0.1)}
    factors = {'L0_conv_qk_w': 8.0,
     'L0_conv_vs_w': 4.281,
     'L0_conv_depth_w': 8.0,
     'L0_conv_fu1_w': 8.0,
     'L0_conv_fu2_w': 8.0,
     'L0_conv_proj_w': 2.827}
    for name, (base, spread) in spreads.items():
        noise = np.random.default_rng([zlib.crc32(name.encode()), seed]).standard_normal(out[name].shape)
        drawn = base * np.exp(spread * noise) if base else spread * noise
        out[name] = jnp.asarray(drawn.astype(out[name].dtype))
    for name, factor in factors.items():
        out[name] = (out[name] * factor).astype(out[name].dtype)
    return out
```

```python
import numpy as np
import concourse.bass as bass
from concourse import mybir
from contextlib import ExitStack

F32 = mybir.dt.float32
ACT = mybir.ActivationFunctionType
ALU = mybir.AluOpType
AX = mybir.AxisListType

B, C, H, W = 4, 96, 128, 128
WS, HEADS = 8, 4
SH = WS // 2
A = C // 2
HD = A // HEADS
SCALE = HD ** -0.5
LN_EPS, BN_EPS = 1e-6, 1e-5
R = C // 4
NS = H // WS
NP = W // WS // 2
K = WS * WS
CH = 4 * W
PX = H * W
XW = W + SH
VW = HD + 1
TAPS = [(k // 3 - 1, k % 3 - 1) for k in range(9)]
PE_TAPS = [0, 2, 6, 8]
DVE_TAPS = [k for k in range(9) if k not in PE_TAPS]
FREE = 1
L1_TAPS = TAPS[:4]


def program(nc, x, out, w):
    ctx = ExitStack()
    with ctx:
        def sb(name, shape):
            return ctx.enter_context(nc.sbuf_tensor(name, shape, F32))

        def sem(name):
            return ctx.enter_context(nc.semaphore(name))

        center = sb("center", [C, C])
        mean_w = sb("mean_w", [C, C])
        ident = sb("ident", [128, 128])
        fold = sb("fold", [C, C])
        spread = sb("spread", [C, C])
        head_mask = sb("head_mask", [C, HEADS])
        pair_mask = sb("pair_mask", [C, 2])
        upper = sb("upper", [C, 1])
        wk = sb("wk", [C, 3 * A])
        wq = sb("wq", [C, 3 * A])
        wvs = sb("wvs", [C, C])
        wv2 = sb("wv2", [C, C])
        projT = sb("projT", [C, C])
        proj_y = sb("proj_y", [C, 2, C])
        proj_yc = sb("proj_yc", [C, 2, C])
        fu1T = sb("fu1T", [C, R])
        fu2T = sb("fu2T", [R, C])
        w1T = sb("w1T", [C, R])
        w2T = sb("w2T", [R, 4, C])
        ln_w = sb("ln_w", [C, 1])
        ln_b = sb("ln_b", [C, 1])
        q_b = sb("q_b", [C, 1])
        k_b = sb("k_b", [C, 1])
        vs_b = sb("vs_b", [C, 1])
        v2_b = sb("v2_b", [C, 1])
        depth_w = sb("depth_w", [C, 9])
        depth_b = sb("depth_b", [C, 1])
        proj_b = sb("proj_b", [C, 1])
        bn = sb("bn", [R, 4])
        b2 = sb("b2", [C, 4])
        l1_b = sb("l1_b", [C, 1])
        eps = sb("eps", [C, 2])
        k_bias = sb("k_bias", [C, HEADS])
        q_bias = sb("q_bias", [C, 2])
        q_scale = sb("q_scale", [C, 2])
        vs_bias = sb("vs_bias", [C, 1])
        y_bias = sb("y_bias", [C, 1])
        bn_scale = sb("bn_scale", [R, 1])

        xc = sb("xc", [C, 2, CH])
        xsum = sb("xsum", [C, CH])
        sq = sb("sq", [C, CH])
        lnv = sb("lnv", [C, CH])
        rstd = sb("rstd", [C, CH])
        xn = sb("xn", [C, WS, XW])
        xw = sb("xw", [C, NP, 2, K])
        kd = sb("kd", [C, NP, HEADS, K])
        qd = sb("qd", [C, NP, 2, K])
        vd = sb("vd", [128, NP, 2, 2, 2, VW])
        sd = sb("sd", [128, 2, 512])
        pr = sb("pr", [128, 2, 512])
        pt = sb("pt", [128, 2, 512])
        mx = sb("mx", [128, 4, 8])
        rec = sb("rec", [128, 2, 16])
        yq = sb("yq", [128, 4, 2, A])
        vsp = sb("vsp", [C, H + 2, W + 2])
        y1 = sb("y1", [C, H, 2, 4 * WS])
        vstat = sb("vstat", [C, 2 * NS])
        ystat = sb("ystat", [C, 2 * NS])

        edge = sb("edge", [C, 24])
        st = sb("st", [C, 32])
        tr = sb("tr", [R, 8])
        tap_w = sb("tap_w", [C, 9])
        l1_w = sb("l1_w", [C, 4])
        z_bias = sb("z_bias", [C, 1])
        diag = sb("diag", [C, len(PE_TAPS), C])

        x0 = sb("x0", [C, 2, WS, W])
        mb = sb("mb", [C, 2, WS, XW])
        zs = sb("zs", [C, 2, WS + 1, W + 2])
        oa = sb("oa", [C, 2, WS, W])
        ob = sb("ob", [C, WS, W])
        oc = sb("oc", [C, WS, W])
        oo = sb("oo", [C, 2, WS, W])

        banks_ln = ctx.enter_context(nc.psum_tensor("banks_ln", [128, 2, 512], F32))
        banks_g = ctx.enter_context(nc.psum_tensor("banks_g", [128, 2, 512], F32))
        banks_s = ctx.enter_context(nc.psum_tensor("banks_s", [128, 2, 512], F32))
        banks_h = ctx.enter_context(nc.psum_tensor("banks_h", [128, 2, 512], F32))
        ps_d, ps_var = banks_ln[:C, 0, :], banks_ln[:C, 1, :]
        ps_tp = banks_h[:, 0, :]
        ps_o = banks_h[:, 1, :]

        w_loaded = sem("w_loaded")
        zeroed = sem("zeroed")
        padded = sem("padded")
        x_loaded = [sem("x_loaded0"), sem("x_loaded1")]
        x0_loaded = [sem("x0_loaded0"), sem("x0_loaded1")]
        stored = [sem("stored0"), sem("stored1")]
        pe_set = sem("pe_set")
        act_set = sem("act_set")
        dve_set = sem("dve_set")
        d_done = sem("d_done")
        sq_done = sem("sq_done")
        var_done = sem("var_done")
        ln_done = sem("ln_done")
        rstd_done = sem("rstd_done")
        xn_done = sem("xn_done")
        xw_done = sem("xw_done")
        xsum_done = sem("xsum_done")
        kq_done = sem("kq_done")
        vt_done = sem("vt_done")
        vs_done = sem("vs_done")
        kd_done = sem("kd_done")
        qd_done = sem("qd_done")
        vd_done = sem("vd_done")
        vsp_done = sem("vsp_done")
        s_done = sem("s_done")
        mx_done = sem("mx_done")
        sd_done = sem("sd_done")
        pr_done = sem("pr_done")
        tp_done = sem("tp_done")
        pt_done = sem("pt_done")
        pv_done = sem("pv_done")
        rec_done = sem("rec_done")
        yq_done = sem("yq_done")
        yt_done = sem("yt_done")
        y1_done = sem("y1_done")
        xsum_zero = sem("xsum_zero")
        mid_to_pe = sem("mid_to_pe")
        mid_dve = sem("mid_dve")
        mid_pe = sem("mid_pe")
        mid_act = sem("mid_act")
        conv_done = sem("conv_done")
        m_step = sem("m_step")
        wrap_done = sem("wrap_done")
        z_done = sem("z_done")
        halo_done = sem("halo_done")
        zs_done = sem("zs_done")
        oa_done = sem("oa_done")
        ob_done = sem("ob_done")
        od_done = sem("od_done")
        oo_done = sem("oo_done")

        LOADS = [
            (center[:], w["center"]), (mean_w[:], w["mean_w"]), (ident[:], w["ident"]),
            (fold[:], w["fold"]), (spread[:], w["spread"]), (head_mask[:], w["head_mask"]),
            (pair_mask[:], w["pair_mask"]), (upper[:], w["upper"]),
            (wk[:, A:2 * A], w["qkT"][:, A:2 * A]), (wq[:, A:2 * A], w["qkT"][:, 0:A]),
            (wvs[:], w["vsT"]), (wv2[:, 0:A], w["vsT"][:, 0:A]), (wv2[:, A:C], w["vsT"][:, 0:A]),
            (projT[:], w["projT"]), (proj_y[0:A, 0, :], w["projT"][0:A, :]),
            (proj_y[A:C, 1, :], w["projT"][0:A, :]),
            (fu1T[:], w["fu1T"]), (fu2T[:], w["fu2T"]), (w1T[:], w["w1T"]), (w2T[:], w["w2T"]),
            (ln_w[:], w["ln_w"]), (ln_b[:], w["ln_b"]),
            (q_b[0:A, :], w["qk_b"][0:A, :]), (q_b[A:C, :], w["qk_b"][0:A, :]),
            (k_b[0:A, :], w["qk_b"][A:C, :]), (k_b[A:C, :], w["qk_b"][A:C, :]),
            (vs_b[:], w["vs_b"]), (v2_b[0:A, :], w["vs_b"][0:A, :]), (v2_b[A:C, :], w["vs_b"][0:A, :]),
            (depth_w[:], w["depth_w"]), (depth_b[:], w["depth_b"]), (proj_b[:], w["proj_b"]),
            (bn[:, 0:1], w["gamma"]), (bn[:, 1:2], w["beta"]), (bn[:, 2:3], w["rmean"]),
            (bn[:, 3:4], w["rvar"]), (b2[:], w["b2"][:, 0:4]), (l1_b[:], w["l1_b"]),
        ]
        N_DVE_SET = 11
        N_MID, MID_STEPS, MID_PE = 38, 8, 8
        N_ZERO = 3
        N_PAD = 9

        def chunk(ap):
            return ap.rearrange("c (r x) -> c r x", x=W)

        def rows_of(i, c):
            return i * WS + SH if c == 0 else (i * WS + WS) % H

        block = ctx.enter_context(nc.Block())

        @block.sync
        def _(sp):
            for s in stored:
                sp.sem_inc(s, FREE)
            def load_x(b, i, c):
                sp.dma_start(chunk(xc[:, c, :]), x[b, :, bass.ds(rows_of(i, c), 4), :]).then_inc(x_loaded[c], 16)

            for c in range(2):
                load_x(0, 0, c)
            sp.wait_ge(zeroed, N_ZERO)
            for dst, src in LOADS:
                sp.dma_start(dst, src).then_inc(w_loaded, 16)

            with sp.Fori(0, B) as b:
                with sp.Fori(0, NS) as i:
                    nxt = b * NS + i + 1
                    s = nxt % (B * NS)
                    img, strip = sp.snap(s // NS), sp.snap(s % NS)
                    for c in range(2):
                        sp.wait_ge(d_done, FREE + 2 * nxt - 1 + c)
                        sp.wait_ge(xsum_done, FREE + 2 * nxt - 1 + c)
                        load_x(img, strip, c)

                def load_x0(j, k):
                    sp.dma_start(x0[:, k, :, :], x[b, :, bass.ds(j * WS, WS), :]).then_inc(x0_loaded[k], 16)

                def store(j, k):
                    sp.wait_ge(oo_done, FREE + b * NS + j + 1)
                    sp.dma_start(out[b, :, bass.ds(j * WS, WS), :], oo[:, k, :, :]).then_inc(stored[k], 16)

                load_x0(0, 0)
                load_x0(1, 1)
                with sp.Fori(0, NS // 2 - 1) as jj:
                    for k in range(2):
                        store(2 * jj + k, k)
                        load_x0(2 * jj + 2 + k, k)
                for k in range(2):
                    store(NS - 2 + k, k)
            for k in range(2):
                sp.wait_ge(stored[k], FREE + 16 * B * NS // 2)

        @block.gpsimd
        def _(pool):
            for s in (xsum_done, oo_done):
                pool.sem_inc(s, FREE)
            for t in (wk, wq, proj_y):
                nc.gpsimd.memset(t[:], 0.0).then_inc(zeroed, 1)
            nc.gpsimd.memset(vsp[:], 0.0).then_inc(padded, 1)
            nc.gpsimd.memset(vd[:], 0.0).then_inc(padded, 1)
            nc.gpsimd.memset(zs[:], 0.0).then_inc(padded, 1)
            nc.gpsimd.memset(edge[:], 0.0).then_inc(padded, 1)
            nc.gpsimd.memset(eps[:, 0:1], LN_EPS).then_inc(padded, 1)
            nc.gpsimd.memset(eps[:, 1:2], BN_EPS).then_inc(padded, 1)
            nc.gpsimd.memset(mb[:], 0.0).then_inc(padded, 1)
            pool.wait_ge(padded, 7)
            for h in range(2):
                nc.gpsimd.memset(vd[h * K:(h + 1) * K, :, :, :, h, HD], 1.0).then_inc(padded, 1)
            pool.wait_ge(padded, N_PAD)

            with pool.Fori(0, B) as b:
                nc.gpsimd.memset(xsum[:], 0.0).then_inc(xsum_zero, 1)
                with pool.Fori(0, NS) as i:
                    t = b * NS + i
                    for c in range(2):
                        pool.wait_ge(x_loaded[c], 16 * (t + 1))
                        pool.wait_ge(xsum_zero, b + 1)
                        if c == 1:
                            pool.wait_ge(vt_done, FREE + t)
                            pool.wait_ge(xn_done, 4 * (t + 1))
                        pool.wait_ge(xsum_done, FREE + 2 * t + c)
                        nc.gpsimd.tensor_tensor(xsum[:], xsum[:], xc[:, c, :], ALU.add).then_inc(xsum_done, 1)
                    for wi in range(2):
                        px = xn[:, :, SH + wi * W // 2:SH + (wi + 1) * W // 2]
                        nc.gpsimd.tensor_copy(xw[:, :, wi, :].rearrange("c p (r x) -> c p r x", x=WS),
                                              px.rearrange("c r (p x) -> c p r x", x=WS)).then_inc(xw_done, 1)
                with pool.Fori(0, NS // 2) as jj:
                    for k in range(2):
                        u = b * NS + 2 * jj + k
                        pool.wait_ge(ob_done, FREE + 2 * (u + 1))
                        nc.gpsimd.tensor_tensor(ob[:], ob[:], oc[:], ALU.add).then_inc(od_done, 1)
                        pool.wait_ge(od_done, u + 1)
                        pool.wait_ge(oa_done, 2 * (u + 1))
                        pool.wait_ge(stored[k], FREE + 16 * (b * (NS // 2) + jj))
                        nc.gpsimd.tensor_tensor(oo[:, k, :, :], ob[:], oa[:, k, :, :], ALU.add).then_inc(oo_done, 1)

        @block.tensor
        def _(pe):
            for s in (vt_done, d_done):
                pe.sem_inc(s, FREE)
            mm = nc.tensor.matmul

            def d_of(s, c):
                pe.wait_ge(x_loaded[c], 16 * (s + 1))
                if not (isinstance(s, int) and s == 0 and c == 0):
                    pe.wait_ge(xn_done, 4 * s + 2 * c)
                mm(ps_d, center[:], xc[:, c, :], start=True, stop=True).then_inc(d_done, 1)

            def var_of(s, c):
                pe.wait_ge(sq_done, 2 * s + c + 1)
                mm(ps_var, mean_w[:], sq[:], start=True, stop=True).then_inc(var_done, 1)

            pe.wait_ge(w_loaded, 16 * len(LOADS))
            bias_ps = banks_s[:C, 0, 0:4]
            mm(bias_ps[:, 0:1], wk[:, A:3 * A], ln_b[:], start=True, stop=False)
            mm(bias_ps[:, 0:1], wk[:, 0:2 * A], ln_b[:], start=False, stop=True).then_inc(pe_set, 1)
            mm(bias_ps[:, 1:2], wq[:, A:3 * A], ln_b[:], start=True, stop=False)
            mm(bias_ps[:, 1:2], wq[:, 0:2 * A], ln_b[:], start=False, stop=True).then_inc(pe_set, 1)
            mm(bias_ps[:, 2:3], wvs[:], ln_b[:], start=True, stop=True).then_inc(pe_set, 1)
            mm(bias_ps[:, 3:4], wv2[:], ln_b[:], start=True, stop=True).then_inc(pe_set, 1)
            for c in range(2):
                d_of(0, c)
                var_of(0, c)
            pe.wait_ge(dve_set, N_DVE_SET)
            pe.wait_ge(padded, N_PAD)

            def phase_a(b, i):
                t = b * NS + i
                win = lambda w: xn[:, :, SH + w * W // 2:SH + (w + 1) * W // 2].rearrange(
                    "c r (p x) -> c p r x", x=WS)

                def scores(q):
                    for e in range(2):
                        p = 2 * q + e
                        last = mm(banks_s[:, q % 2, e * 256:(e + 1) * 256],
                                  qd[:, p, :, :].rearrange("c w k -> c (w k)"),
                                  kd[:, p, :, :].rearrange("c h k -> c (h k)"), start=True, stop=True)
                    last.then_inc(s_done, 1)

                def transposes(q):
                    pe.wait_ge(pr_done, FREE + 4 * t + q + 1)
                    if q == 0:
                        pe.wait_ge(vd_done, 4 * (t + 1))
                    else:
                        pe.wait_ge(pt_done, 4 * t + q)
                    for j in range(4):
                        last = nc.tensor.transpose(ps_tp[:, j * 128:(j + 1) * 128],
                                                   pr[:, q % 2, j * 128:(j + 1) * 128], ident[:])
                    last.then_inc(tp_done, 1)

                def values(q):
                    pe.wait_ge(pt_done, 4 * t + (q + 1 if q < 2 else 4))
                    bank = ps_o if q < 2 else ps_tp
                    for j in range(4):
                        at = (q % 2) * 208 + j * 52
                        last = mm(bank[:, at:at + 52], pt[:, q % 2, j * 128:(j + 1) * 128],
                                  vd[:, 2 * q + j // 2, j % 2, :, :, :].rearrange("k w h d -> k (w h d)"),
                                  start=True, stop=True)
                    last.then_inc(pv_done, 1)

                pe.wait_ge(xn_done, 4 * (t + 1))
                pe.wait_ge(vsp_done, FREE + 2 * t)
                for n, wt in enumerate((wk, wq)):
                    mm(banks_g[:C, n, :], wt[:, A:3 * A], win(0), start=True, stop=False)
                    mm(banks_g[:C, n, :], wt[:, 0:2 * A], win(1), start=False, stop=True).then_inc(kq_done, 1)
                pe.wait_ge(xw_done, 2 * (t + 1))
                pe.wait_ge(yq_done, FREE + 4 * t)
                for p in range(NP):
                    lhs = xw[:, p, :, :].rearrange("c w k -> c (w k)")
                    last = mm(ps_tp[:, p * A:(p + 1) * A], lhs, wvs[:, 0:A], start=True, stop=True)
                last.then_inc(vt_done, 1)
                d_of(t + 1, 0)
                pe.wait_ge(kd_done, 4 * (t + 1))
                mm(banks_g[:C, 0, :], wvs[:], xn[:, 0:4, 0:W], start=True, stop=True).then_inc(vs_done, 1)
                pe.wait_ge(qd_done, 2 * (t + 1))
                mm(banks_g[:C, 1, :], wvs[:], xn[:, 4:8, 0:W], start=True, stop=True).then_inc(vs_done, 1)
                pe.wait_ge(sd_done, FREE + 4 * t)
                pe.wait_ge(zs_done, FREE + 2 * NS * b)
                scores(0)
                scores(1)
                var_of(t + 1, 0)
                transposes(0)
                pe.wait_ge(sd_done, FREE + 4 * t + 1)
                scores(2)
                transposes(1)
                pe.wait_ge(sd_done, FREE + 4 * t + 2)
                scores(3)
                d_of(t + 1, 1)
                pe.wait_ge(y1_done, FREE + 2 * t)
                values(0)
                values(1)
                transposes(2)
                var_of(t + 1, 1)
                transposes(3)
                values(2)
                values(3)
                pe.wait_ge(yq_done, FREE + 4 * (t + 1))
                for e in range(4):
                    last = nc.tensor.transpose(ps_o[:C, e * 128:(e + 1) * 128],
                                               yq[:, e, :, :].rearrange("q g c -> q (g c)"), ident[:])
                last.then_inc(yt_done, 1)

            def between(b):
                one = banks_s[:, 0, :]
                for lhs, rhs, at, m, dve in (
                    (fold[:], st[:, 0:1], 0, C, 1),
                    (fu1T[:], st[:, 5:6], 1, R, 2),
                    (fu2T[:], tr[:, 1:2], 2, C, 3),
                    (spread[:], st[:, 9:10], 3, C, 4),
                    (projT[:], st[:, 12:13], 4, C, 5),
                    (projT[:], st[:, 13:14], 5, C, 5),
                    (w1T[:], st[:, 14:15], 6, R, 6),
                ):
                    pe.wait_ge(mid_to_pe, MID_STEPS * b + dve)
                    mm(one[0:m, at:at + 1], lhs, rhs, start=True, stop=True).then_inc(mid_pe, 1)
                pe.wait_ge(mid_to_pe, MID_STEPS * b + 7)
                for k in range(4):
                    last = mm(one[0:C, 8 + k:9 + k], w2T[:, k, :], tr[:, 5:6], start=True, stop=True)
                last.then_inc(mid_pe, 1)

            def conv(b, j, k, first):
                if k == 0:
                    bank = banks_g
                else:
                    bank = banks_h
                if first:
                    pe.wait_ge(mid_to_pe, MID_STEPS * (b + 1))
                else:
                    pe.wait_ge(m_step, len(DVE_TAPS) * (b * NS + j - 2) + 1)
                for c in range(2):
                    for n, tap in enumerate(PE_TAPS):
                        dh, dw = TAPS[tap]
                        last = mm(bank[:C, c, :], diag[:, n, :],
                                  vsp[:, bass.ds(j * WS + 4 * c + 1 + dh, 4), 1 + dw:1 + dw + W],
                                  start=n == 0, stop=n == len(PE_TAPS) - 1)
                last.then_inc(conv_done, 1)

            def project(b, j, k):
                u = b * NS + j
                pe.wait_ge(wrap_done, u + 1)
                pe.wait_ge(zs_done, FREE + 2 * u)
                for c in range(2):
                    z = banks_s[:C, c, :]
                    mm(z, projT[:], mb[:, k, 4 * c:4 * c + 4, SH:XW], start=True, stop=False)
                    yrow = (j * WS + H - SH) % H if c == 0 else j * WS
                    zr = chunk(z).rearrange("c r (w g x) -> c r w g x", w=2, g=2)
                    for g in range(2):
                        last = mm(zr[:, :, :, g, :], proj_yc[:, g, :], y1[:, bass.ds(yrow, 4), :, :],
                                  start=False, stop=g == 1)
                last.then_inc(z_done, 1)

            with pe.Fori(0, B) as b:
                with pe.Fori(0, NS) as i:
                    phase_a(b, i)
                between(b)
                conv(b, 0, 0, True)
                conv(b, 1, 1, True)
                project(b, 0, 0)
                with pe.Fori(0, NS // 2 - 1) as jj:
                    conv(b, 2 * jj + 2, 0, False)
                    project(b, 2 * jj + 1, 1)
                    conv(b, 2 * jj + 3, 1, False)
                    project(b, 2 * jj + 2, 0)
                project(b, NS - 1, 1)

        @block.scalar
        def _(act):
            for s in (vsp_done, pr_done, y1_done, ob_done):
                act.sem_inc(s, FREE)
            fn = nc.scalar.activation
            act.preload_act_table_set("natural_log_exp_and_others")

            def square(s, c):
                act.wait_ge(d_done, FREE + 2 * s + c + 1)
                fn(sq[:], ps_d, ACT.Square).then_inc(sq_done, 1)

            def rsqrt(s, c):
                act.wait_ge(var_done, 2 * s + c + 1)
                fn(lnv[:], ps_var, ACT.Ln, bias=eps[:, 0:1]).then_inc(ln_done, 1)
                act.wait_ge(ln_done, 2 * s + c + 1)
                fn(rstd[:], lnv[:], ACT.Exp, scale=-0.5).then_inc(rstd_done, 1)

            act.wait_ge(padded, N_PAD)
            for c in range(2):
                square(0, c)
                rsqrt(0, c)
            act.wait_ge(w_loaded, 16 * len(LOADS))
            fn(bn_scale[:], bn[:, 3:4], ACT.Ln, bias=eps[:R, 1:2]).then_inc(act_set, 1)
            act.wait_ge(act_set, 1)
            fn(bn_scale[:], bn_scale[:], ACT.Exp, scale=-0.5).then_inc(act_set, 1)
            act.wait_ge(dve_set, N_DVE_SET)

            def phase_a(b, i):
                t = b * NS + i
                act.wait_ge(kq_done, 2 * t + 1)
                for h in range(HEADS):
                    fn(kd[:, :, h, :], banks_g[:C, 0, :].rearrange("c (p k) -> c p k", k=K), ACT.Identity,
                       bias=k_bias[:, h:h + 1], scale=head_mask[:, h:h + 1]).then_inc(kd_done, 1)
                square(t + 1, 0)
                act.wait_ge(vt_done, FREE + t + 1)
                for wi in range(2):
                    for h in range(2):
                        src = ps_tp[wi * K:(wi + 1) * K, 0:NP * A].rearrange("k (p s h d) -> k p s h d", s=2, h=2, d=HD)
                        fn(vd[h * K:(h + 1) * K, :, :, wi, h, 0:HD], src[:, :, :, h, :], ACT.Copy).then_inc(vd_done, 1)
                for c in range(2):
                    act.wait_ge(vs_done, 2 * t + c + 1)
                    fn(vsp[:, bass.ds(rows_of(i, c) + 1, 4), 1:1 + W], chunk(banks_g[:C, c, :]), ACT.Identity,
                       bias=vs_bias[:], accum_out=vstat[:, bass.ds(2 * i + c, 1)]).then_inc(vsp_done, 1)
                rsqrt(t + 1, 0)

                def exps(q):
                    act.wait_ge(sd_done, FREE + 4 * t + q + 1)
                    fn(pr[:, q % 2, :], sd[:, q % 2, :], ACT.Exp).then_inc(pr_done, 1)

                def transposed(q):
                    act.wait_ge(tp_done, 4 * t + q + 1)
                    fn(pt[:, q % 2, :], ps_tp[:, :], ACT.Copy).then_inc(pt_done, 1)

                exps(0)
                exps(1)
                transposed(0)
                exps(2)
                transposed(1)
                exps(3)
                square(t + 1, 1)
                transposed(2)
                rsqrt(t + 1, 1)
                transposed(3)
                act.wait_ge(yt_done, t + 1)
                src = ps_o[:C, :].rearrange("c (e w r x) -> c e w r x", e=4, w=2, x=WS)
                for wi in range(2):
                    dst = y1[:, bass.ds(i * WS, WS), wi, :].rearrange("c r (e x) -> c e r x", x=WS)
                    fn(dst, src[:, :, wi, :, :], ACT.Identity, bias=y_bias[:],
                       accum_out=ystat[:, bass.ds(2 * i + wi, 1)]).then_inc(y1_done, 1)

            def phase_b(b, j, k):
                u = b * NS + j
                act.wait_ge(m_step, len(DVE_TAPS) * (u + 1))
                fn(mb[:, k, :, W:XW], mb[:, k, :, 0:SH], ACT.Copy).then_inc(wrap_done, 1)

            def taps(b, j, k):
                u = b * NS + j
                act.wait_ge(zs_done, FREE + 2 * (u + 1))
                act.wait_ge(oo_done, FREE + u)
                for n, (o, tap) in enumerate(((ob, 2), (oc, 3))):
                    dh, dw = L1_TAPS[tap]
                    fn(o[:], zs[:, k, 1 + dh:1 + dh + WS, 1 + dw:1 + dw + W], ACT.Copy,
                       scale=l1_w[:, tap:tap + 1]).then_inc(ob_done, 1)

            with act.Fori(0, B) as b:
                with act.Fori(0, NS) as i:
                    phase_a(b, i)
                act.wait_ge(mid_pe, MID_PE * b + 3)
                fn(st[:, 6:7], banks_s[:C, 0, 2:3], ACT.Exp, scale=-1.0).then_inc(mid_act, 1)
                phase_b(b, 0, 0)
                with act.Fori(0, NS // 2 - 1) as jj:
                    phase_b(b, 2 * jj + 1, 1)
                    taps(b, 2 * jj, 0)
                    phase_b(b, 2 * jj + 2, 0)
                    taps(b, 2 * jj + 1, 1)
                phase_b(b, NS - 1, 1)
                taps(b, NS - 2, 0)
                taps(b, NS - 1, 1)

        @block.vector
        def _(dve):
            for s in (yq_done, sd_done, zs_done):
                dve.sem_inc(s, FREE)
            v = nc.vector

            def normalise(s, c):
                dve.wait_ge(rstd_done, 2 * s + c + 1)
                d, r = chunk(ps_d), chunk(rstd[:])
                rows = xn[:, 4 * c:4 * c + 4, :]
                v.tensor_tensor(rows[:, :, 0:W], d, r, ALU.mult).then_inc(xn_done, 1)
                v.tensor_tensor(rows[:, :, W:XW], d[:, :, 0:SH], r[:, :, 0:SH], ALU.mult).then_inc(xn_done, 1)

            for c in range(2):
                normalise(0, c)
            dve.wait_ge(pe_set, 4)
            bias_ps = banks_s[:C, 0, 0:4]
            n = [0]

            def setup(ins):
                ins.then_inc(dve_set, 1)
                n[0] += 1
                dve.wait_ge(dve_set, n[0])

            dve.wait_ge(w_loaded, 16 * len(LOADS))
            for t, width in ((wk, 3 * A), (wq, 3 * A), (wvs, C)):
                setup(v.tensor_scalar(t[:], t[:], ln_w[:], None, ALU.mult))
            setup(v.tensor_tensor(k_b[:], bias_ps[:, 0:1], k_b[:], ALU.add))
            setup(v.tensor_tensor(q_b[:], bias_ps[:, 1:2], q_b[:], ALU.add))
            setup(v.tensor_tensor(vs_bias[:], bias_ps[:, 2:3], vs_b[:], ALU.add))
            setup(v.tensor_tensor(y_bias[:], bias_ps[:, 3:4], v2_b[:], ALU.add))
            setup(v.tensor_scalar(k_bias[:], head_mask[:], k_b[:], None, ALU.mult))
            setup(v.tensor_scalar(q_bias[:], pair_mask[:], q_b[:], SCALE, ALU.mult, ALU.mult))
            setup(v.tensor_scalar(q_scale[:], pair_mask[:], SCALE, None, ALU.mult))
            dve.wait_ge(act_set, 2)
            setup(v.tensor_tensor(bn_scale[:], bn_scale[:], bn[:, 0:1], ALU.mult))
            assert n[0] == N_DVE_SET

            def phase_a(b, i):
                t = b * NS + i
                dve.wait_ge(kq_done, 2 * t + 2)
                for wi in range(2):
                    v.tensor_scalar(qd[:, :, wi, :], banks_g[:C, 1, :].rearrange("c (p k) -> c p k", k=K),
                                    q_scale[:, wi:wi + 1], q_bias[:, wi:wi + 1], ALU.mult, ALU.add).then_inc(qd_done, 1)

                def softmax(q):
                    dve.wait_ge(s_done, 4 * t + q + 1)
                    s = banks_s[:, q % 2, :].rearrange("p (g k) -> p g k", k=K)
                    v.tensor_reduce(mx[:, q, :], s, AX.X, ALU.max).then_inc(mx_done, 1)
                    dve.wait_ge(mx_done, 4 * t + q + 1)
                    if q < 2:
                        dve.wait_ge(pr_done, FREE + 4 * t)
                    else:
                        dve.wait_ge(pr_done, FREE + 4 * t + q - 1)
                    v.tensor_tensor(sd[:, q % 2, :].rearrange("p (g k) -> p g k", k=K), s,
                                    mx[:, q, :].unsqueeze(2).to_broadcast([128, 8, K]),
                                    ALU.subtract).then_inc(sd_done, 1)

                def divide(half):
                    dve.wait_ge(pv_done, 4 * t + 2 * half + 2)
                    bank = ps_o if half == 0 else ps_tp
                    o = bank[:, 0:416].rearrange("q (n w h d) -> q n w h d", w=2, h=2, d=VW)
                    for wi in range(2):
                        r = slice(wi * K, (wi + 1) * K)
                        rc = rec[r, half, :].rearrange("q (n h) -> q n h", h=2)
                        v.reciprocal(rc, o[r, :, wi, :, HD]).then_inc(rec_done, 1)
                    for wi in range(2):
                        dve.wait_ge(rec_done, 4 * t + 2 * half + wi + 1)
                        r = slice(wi * K, (wi + 1) * K)
                        rc = rec[r, half, :].rearrange("q (n h) -> q n h", h=2)
                        v.tensor_tensor(yq[r, :, half, :].rearrange("q e (s h d) -> q e s h d", s=2, d=HD),
                                        o[r, :, wi, :, 0:HD].rearrange("q (e s) h d -> q e s h d", s=2), rc.rearrange("q (e s) h -> q e s h", s=2).unsqueeze(4).to_broadcast([K, 4, 2, 2, HD]),
                                        ALU.mult).then_inc(yq_done, 1)

                softmax(0)
                softmax(1)
                normalise(t + 1, 0)
                softmax(2)
                softmax(3)
                divide(0)
                normalise(t + 1, 1)
                divide(1)

            def between(b):
                n = [0]

                def step(ins):
                    ins.then_inc(mid_dve, 1)
                    n[0] += 1
                    dve.wait_ge(mid_dve, N_MID * b + n[0])

                def to_pe(ins):
                    ins.then_inc(mid_to_pe, 1)
                    k[0] += 1
                    dve.wait_ge(mid_to_pe, MID_STEPS * b + k[0])

                k = [0]
                one = banks_s[:, 0, :]
                s = lambda i, w=1: st[:, i:i + w]
                img = vsp[:, 1:1 + H, 1:1 + W]
                dve.wait_ge(ob_done, FREE + 2 * NS * b)
                dve.wait_ge(y1_done, FREE + 2 * NS * (b + 1))
                dve.wait_ge(vsp_done, FREE + 2 * NS * (b + 1))
                dve.wait_ge(xsum_done, FREE + 2 * NS * (b + 1))
                to_pe(v.tensor_reduce(s(0), ystat[:], AX.X, ALU.add))
                step(v.tensor_reduce(s(1), vstat[:], AX.X, ALU.add))
                step(v.tensor_reduce(s(2), xsum[:], AX.X, ALU.add))
                for at, rows in ((0, H - 1), (2, 0)):
                    step(v.tensor_reduce(edge[:, at:at + 1], img[:, rows, :], AX.X, ALU.add))
                    step(v.tensor_reduce(edge[:, 3 + at:4 + at], img[:, :, rows], AX.X, ALU.add))
                    for bt, cols in ((0, W - 1), (2, 0)):
                        step(v.tensor_copy(edge[:, 6 + 3 * at + bt:7 + 3 * at + bt], img[:, rows, cols:cols + 1]))
                e3 = edge[:, 6:15].rearrange("c (a b) -> c a b", b=3)
                sums = edge[:, 15:24].rearrange("c (a b) -> c a b", b=3)
                step(v.tensor_tensor(sums, e3, edge[:, 0:3].unsqueeze(2).to_broadcast([C, 3, 3]), ALU.subtract))
                step(v.tensor_tensor(sums, sums, edge[:, 3:6].unsqueeze(1).to_broadcast([C, 3, 3]), ALU.subtract))
                step(v.tensor_scalar(edge[:, 15:24], edge[:, 15:24], s(1), 1.0 / PX, ALU.add, ALU.mult))
                step(v.tensor_tensor(edge[:, 15:24], edge[:, 15:24], depth_w[:], ALU.mult))
                step(v.tensor_reduce(s(3), edge[:, 15:24], AX.X, ALU.add))
                step(v.tensor_tensor(s(3), s(3), depth_b[:], ALU.add))
                step(v.tensor_tensor(s(4), s(1), upper[:], ALU.mult))
                dve.wait_ge(mid_pe, MID_PE * b + 1)
                step(v.tensor_tensor(s(4), one[:C, 0:1], s(4), ALU.add))
                step(v.tensor_scalar(s(4), s(4), 1.0 / PX, None, ALU.mult))
                to_pe(v.tensor_tensor(s(5), s(4), s(3), ALU.add))
                dve.wait_ge(mid_pe, MID_PE * b + 2)
                step(v.tensor_scalar(tr[:, 0:1], one[:R, 1:2], 0.2, None, ALU.mult))
                to_pe(v.tensor_tensor(tr[:, 1:2], one[:R, 1:2], tr[:, 0:1], ALU.max))
                dve.wait_ge(mid_act, b + 1)
                step(v.tensor_scalar(s(7), s(6), 1.0, None, ALU.add))
                to_pe(v.reciprocal(s(9), s(7)))
                step(v.tensor_scalar(s(10), s(9), -1.0, 1.0, ALU.mult, ALU.add))
                step(v.tensor_tensor(s(11), s(4), s(9), ALU.mult))
                step(v.scalar_tensor_tensor(out=s(12), in0=s(3), scalar=s(10), in1=s(11), op0=ALU.mult, op1=ALU.add))
                to_pe(v.tensor_tensor(s(13), depth_b[:], s(10), ALU.mult))
                dve.wait_ge(mid_pe, MID_PE * b + 6)
                step(v.tensor_tensor(s(15), one[:C, 4:5], proj_b[:], ALU.add))
                to_pe(v.scalar_tensor_tensor(out=s(14), in0=s(2), scalar=1.0 / PX, in1=s(15), op0=ALU.mult, op1=ALU.add))
                dve.wait_ge(mid_pe, MID_PE * b + 7)
                step(v.tensor_copy(s(17), one[:C, 3:4]))
                step(v.tensor_tensor(z_bias[:], one[:C, 5:6], proj_b[:], ALU.add))
                step(v.tensor_tensor(tr[:, 3:4], one[:R, 6:7], bn[:, 2:3], ALU.subtract))
                step(v.scalar_tensor_tensor(out=tr[:, 4:5], in0=tr[:, 3:4], scalar=bn_scale[:], in1=bn[:, 1:2],
                                            op0=ALU.mult, op1=ALU.add))
                to_pe(v.tensor_scalar(tr[:, 5:6], tr[:, 4:5], 0.0, None, ALU.max))
                step(v.tensor_scalar(tap_w[:], depth_w[:], s(10), None, ALU.mult))
                step(v.tensor_tensor(s(16), s(9), upper[:], ALU.mult))
                step(v.tensor_tensor(tap_w[:, 4:5], tap_w[:, 4:5], s(16), ALU.add))
                step(v.tensor_scalar(proj_yc[:].rearrange("c g o -> c (g o)"), proj_y[:].rearrange("c g o -> c (g o)"),
                                     s(17), None, ALU.mult))
                for m, tap in enumerate(PE_TAPS):
                    step(v.tensor_scalar(diag[:, m, :], ident[:C, :C], tap_w[:, tap:tap + 1], None, ALU.mult))
                step(v.memset(zs[:, 1, WS, :], 0.0))
                dve.wait_ge(mid_pe, MID_PE * (b + 1))
                to_pe(v.tensor_tensor(l1_w[:], one[:C, 8:12], b2[:], ALU.add))
                assert (n[0], k[0]) == (N_MID, MID_STEPS), (n[0], k[0])

            def mix(b, j, k):
                u = b * NS + j
                bank = banks_g if k == 0 else banks_h
                dve.wait_ge(conv_done, u + 1)
                for n, tap in enumerate(DVE_TAPS):
                    dh, dw = TAPS[tap]
                    acc = mb[:, k, :, 0:W]
                    if n:
                        dve.wait_ge(m_step, len(DVE_TAPS) * u + n)
                    src = bank[:C, :, :].rearrange("c a (r x) -> c (a r) x", x=W) if n == 0 else acc
                    v.scalar_tensor_tensor(out=acc, in0=vsp[:, bass.ds(j * WS + 1 + dh, WS), 1 + dw:1 + dw + W],
                                           scalar=tap_w[:, tap:tap + 1], in1=src,
                                           op0=ALU.mult, op1=ALU.add).then_inc(m_step, 1)

            def residual(b, j, jj, k):
                u = b * NS + j
                dve.wait_ge(z_done, u + 1)
                dve.wait_ge(x0_loaded[k], 16 * (b * (NS // 2) + jj + 1))
                v.tensor_copy(zs[:, k, 0, :], zs[:, 1 - k, WS, :]).then_inc(halo_done, 1)
                z = banks_s[:C, :, :].rearrange("c a (r x) -> c (a r) x", x=W)
                v.scalar_tensor_tensor(out=zs[:, k, 1:1 + WS, 1 + SH:1 + W], in0=z[:, :, 0:W - SH], scalar=z_bias[:],
                                       in1=x0[:, k, :, SH:W], op0=ALU.add, op1=ALU.add).then_inc(zs_done, 1)
                v.scalar_tensor_tensor(out=zs[:, k, 1:1 + WS, 1:1 + SH], in0=z[:, :, W - SH:W], scalar=z_bias[:],
                                       in1=x0[:, k, :, 0:SH], op0=ALU.add, op1=ALU.add).then_inc(zs_done, 1)

            def taps(b, j, k):
                u = b * NS + j
                dve.wait_ge(zs_done, FREE + 2 * (u + 1))
                dve.wait_ge(halo_done, u + 1)
                for n in range(2):
                    dh, dw = L1_TAPS[n]
                    src = zs[:, k, 1 + dh:1 + dh + WS, 1 + dw:1 + dw + W]
                    if n == 0:
                        ins = v.tensor_scalar(oa[:, k, :, :], src, l1_w[:, 0:1], l1_b[:], ALU.mult, ALU.add)
                    else:
                        dve.wait_ge(oa_done, 2 * u + 1)
                        ins = v.scalar_tensor_tensor(out=oa[:, k, :, :], in0=src, scalar=l1_w[:, 1:2],
                                                     in1=oa[:, k, :, :], op0=ALU.mult, op1=ALU.add)
                    ins.then_inc(oa_done, 1)

            def finish(b, j, jj, k):
                u = b * NS + j
                ago = NS * b if isinstance(j, int) and j == 0 else u - 1
                dve.wait_ge(ob_done, FREE + 2 * ago)
                dve.wait_ge(oo_done, FREE + ago)
                residual(b, j, jj, k)
                taps(b, j, k)

            with dve.Fori(0, B) as b:
                with dve.Fori(0, NS) as i:
                    phase_a(b, i)
                between(b)
                mix(b, 0, 0)
                mix(b, 1, 1)
                finish(b, 0, 0, 0)
                with dve.Fori(0, NS // 2 - 1) as jj:
                    mix(b, 2 * jj + 2, 0)
                    finish(b, 2 * jj + 1, jj, 1)
                    mix(b, 2 * jj + 3, 1)
                    finish(b, 2 * jj + 2, jj + 1, 0)
                finish(b, NS - 1, NS // 2 - 1, 1)


def kernel(**inputs):
    import concourse.bacc as bacc
    from concourse.bass_utils import run_bass_kernel_spmd

    arr = {k: np.asarray(v) for k, v in inputs.items()}
    l0 = {k[len("L0_conv_"):]: v for k, v in arr.items() if k.startswith("L0_conv_")}
    l1 = {k[len("L1_conv_"):]: v for k, v in arr.items() if k.startswith("L1_conv_")}
    col = lambda a: a.reshape(-1, 1)
    row = np.arange(C)
    w = {
        "center": np.eye(C) - 1.0 / C,
        "mean_w": np.full((C, C), 1.0 / C),
        "ident": np.eye(128),
        "fold": row[:, None] % A == row[None, :],
        "spread": row[:, None] == row[None, :] % A,
        "head_mask": (row[:, None] % A) // HD == np.arange(HEADS)[None, :],
        "pair_mask": row[:, None] // A == np.arange(2)[None, :],
        "upper": row[:, None] >= A,
    }
    w = {k: v.astype(np.float32) for k, v in w.items()}
    w |= {
        "qkT": l0["qk_w"].T, "vsT": l0["vs_w"].T, "projT": l0["proj_w"].T,
        "fu1T": l0["fu1_w"].T, "fu2T": l0["fu2_w"].T, "w1T": l1["w1"].T,
        "w2T": l1["w2"].reshape(C, 9, R)[:, 0:4].transpose(2, 1, 0),
        "ln_w": col(l0["ln_w"]), "ln_b": col(l0["ln_b"]), "qk_b": col(l0["qk_b"]), "vs_b": col(l0["vs_b"]),
        "depth_w": l0["depth_w"].reshape(C, 9), "depth_b": col(l0["depth_b"]), "proj_b": col(l0["proj_b"]),
        "gamma": col(l1["gamma"]), "beta": col(l1["beta"]), "rmean": col(l1["running_mean"]),
        "rvar": col(l1["running_var"]), "b2": l1["b2"].reshape(C, 9), "l1_b": col(l1["bias"]),
    }
    arrays = {"in_x": arr["x"].reshape(B, C, H, W)} | {f"in_{k}": v for k, v in w.items()}
    arrays = {k: np.ascontiguousarray(v) for k, v in arrays.items()}

    nc = bacc.Bacc("TRN2", target_bir_lowering=False, num_devices=1)
    dram = {k: nc.dram_tensor(k, v.shape, F32, kind="ExternalInput").ap() for k, v in arrays.items()}
    out = nc.dram_tensor("out_0", (B, C, H, W), F32, kind="ExternalOutput").ap()
    program(nc, dram["in_x"], out, {k[3:]: v for k, v in dram.items()})
    return run_bass_kernel_spmd(nc, [arrays], core_ids=[0]).results[0]["out_0"]
```

```python
import numpy as np
import concourse.bass as bass
from concourse import mybir
from contextlib import ExitStack

F32 = mybir.dt.float32
ACT = mybir.ActivationFunctionType
ALU = mybir.AluOpType
AX = mybir.AxisListType

B, C, H, W = 4, 96, 128, 128
WS, HEADS = 8, 4
SH = WS // 2
A = C // 2
HD = A // HEADS
SCALE = HD ** -0.5
LN_EPS, BN_EPS = 1e-6, 1e-5
R = C // 4
NS = H // WS
NP = W // WS // 2
K = WS * WS
CH = 4 * W
PX = H * W
XW = W + SH
VW = HD + 1
TAPS = [(k // 3 - 1, k % 3 - 1) for k in range(9)]
PE_TAPS = [0, 2, 6, 8]
DVE_TAPS = [k for k in range(9) if k not in PE_TAPS]
FREE = 1
L1_TAPS = TAPS[:4]


def program(nc, x, out, w):
    ctx = ExitStack()
    with ctx:
        def sb(name, shape):
            return ctx.enter_context(nc.sbuf_tensor(name, shape, F32))

        def sem(name):
            return ctx.enter_context(nc.semaphore(name))

        center = sb("center", [C, C])
        mean_w = sb("mean_w", [C, C])
        ident = sb("ident", [128, 128])
        fold = sb("fold", [C, C])
        spread = sb("spread", [C, C])
        head_mask = sb("head_mask", [C, HEADS])
        pair_mask = sb("pair_mask", [C, 2])
        upper = sb("upper", [C, 1])
        wk = sb("wk", [C, 3 * A])
        wq = sb("wq", [C, 3 * A])
        wvs = sb("wvs", [C, C])
        wv2 = sb("wv2", [C, C])
        projT = sb("projT", [C, C])
        proj_y = sb("proj_y", [C, 2, C])
        proj_yc = sb("proj_yc", [C, 2, C])
        fu1T = sb("fu1T", [C, R])
        fu2T = sb("fu2T", [R, C])
        w1T = sb("w1T", [C, R])
        w2T = sb("w2T", [R, 4, C])
        ln_w = sb("ln_w", [C, 1])
        ln_b = sb("ln_b", [C, 1])
        q_b = sb("q_b", [C, 1])
        k_b = sb("k_b", [C, 1])
        vs_b = sb("vs_b", [C, 1])
        v2_b = sb("v2_b", [C, 1])
        depth_w = sb("depth_w", [C, 9])
        depth_b = sb("depth_b", [C, 1])
        proj_b = sb("proj_b", [C, 1])
        bn = sb("bn", [R, 4])
        b2 = sb("b2", [C, 4])
        l1_b = sb("l1_b", [C, 1])
        eps = sb("eps", [C, 2])
        k_bias = sb("k_bias", [C, HEADS])
        q_bias = sb("q_bias", [C, 2])
        q_scale = sb("q_scale", [C, 2])
        vs_bias = sb("vs_bias", [C, 1])
        y_bias = sb("y_bias", [C, 1])
        bn_scale = sb("bn_scale", [R, 1])

        xc = sb("xc", [C, 2, CH])
        sq = sb("sq", [C, CH])
        lnv = sb("lnv", [C, CH])
        rstd = sb("rstd", [C, CH])
        xn = sb("xn", [C, 2, WS, XW])
        xw = sb("xw", [C, NP, 2, K])
        kd = sb("kd", [C, NP, HEADS, K])
        qd = sb("qd", [C, NP, 2, K])
        vd = sb("vd", [128, 2, NP, 2, 2, 2, VW])
        sd = sb("sd", [128, 2, 512])
        mx = sb("mx", [128, 4, 8])
        rec = sb("rec", [128, 2, 16])
        yq = sb("yq", [128, 4, 2, A])
        vsp = sb("vsp", [C, H + 2, W + 2])
        y1 = sb("y1", [C, H, 2, 4 * WS])
        vstat = sb("vstat", [C, 2 * NS])
        ystat = sb("ystat", [C, 2 * NS])
        xstat = sb("xstat", [C, 2 * (B * NS + 2)])

        edge = sb("edge", [C, 24])
        st = sb("st", [C, 32])
        tr = sb("tr", [R, 8])
        tap_w = sb("tap_w", [C, 9])
        l1_w = sb("l1_w", [C, 4])
        z_bias = sb("z_bias", [C, 1])
        diag = sb("diag", [C, len(PE_TAPS), C])

        x0 = sb("x0", [C, 2, WS, W])
        mixed = sb("mixed", [128, 2, WS, XW])
        mb = mixed[:C, :, :, :]
        room = mixed[:].rearrange("p k r x -> p (k r x)")
        pr = room[:, 0:1024].rearrange("p (k n) -> p k n", k=2)
        pt = room[:, 1024:2048].rearrange("p (k n) -> p k n", k=2)
        zs = sb("zs", [C, 2, WS + 1, W + 2])
        oa = sb("oa", [C, 2, WS, W])
        ob = sb("ob", [C, WS, W])
        oc = sb("oc", [C, WS, W])
        oo = sb("oo", [C, 2, WS, W])

        banks_ln = ctx.enter_context(nc.psum_tensor("banks_ln", [128, 2, 512], F32))
        banks_g = ctx.enter_context(nc.psum_tensor("banks_g", [128, 2, 512], F32))
        banks_s = ctx.enter_context(nc.psum_tensor("banks_s", [128, 2, 512], F32))
        banks_h = ctx.enter_context(nc.psum_tensor("banks_h", [128, 2, 512], F32))
        ps_d, ps_var = banks_ln[:C, 0, :], banks_ln[:C, 1, :]
        ps_tp = banks_h[:, 0, :]
        ps_o = banks_h[:, 1, :]

        w_loaded = sem("w_loaded")
        zeroed = sem("zeroed")
        padded = sem("padded")
        x_loaded = [sem("x_loaded0"), sem("x_loaded1")]
        x0_loaded = [sem("x0_loaded0"), sem("x0_loaded1")]
        stored = [sem("stored0"), sem("stored1")]
        pe_set = sem("pe_set")
        act_set = sem("act_set")
        dve_set = sem("dve_set")
        d_done = sem("d_done")
        sq_done = sem("sq_done")
        var_done = sem("var_done")
        ln_done = sem("ln_done")
        rstd_done = sem("rstd_done")
        xn_done = sem("xn_done")
        xw_done = sem("xw_done")
        xsum_done = sem("xsum_done")
        kq_done = sem("kq_done")
        vt_done = sem("vt_done")
        vs_done = sem("vs_done")
        kd_done = sem("kd_done")
        qd_done = sem("qd_done")
        vd_done = sem("vd_done")
        vsp_done = sem("vsp_done")
        s_done = sem("s_done")
        mx_done = sem("mx_done")
        sd_done = sem("sd_done")
        pr_done = sem("pr_done")
        tp_done = sem("tp_done")
        pt_done = sem("pt_done")
        pv_done = sem("pv_done")
        rec_done = sem("rec_done")
        yq_done = sem("yq_done")
        yt_done = sem("yt_done")
        y1_done = sem("y1_done")
        mid_to_pe = sem("mid_to_pe")
        mid_dve = sem("mid_dve")
        mid_pe = sem("mid_pe")
        mid_act = sem("mid_act")
        conv_done = sem("conv_done")
        m_step = sem("m_step")
        wrap_done = sem("wrap_done")
        z_done = sem("z_done")
        halo_done = sem("halo_done")
        zs_done = sem("zs_done")
        oa_done = sem("oa_done")
        ob_done = sem("ob_done")
        od_done = sem("od_done")
        oo_done = sem("oo_done")

        LOADS = [
            (center[:], w["center"]), (mean_w[:], w["mean_w"]), (ident[:], w["ident"]),
            (fold[:], w["fold"]), (spread[:], w["spread"]), (head_mask[:], w["head_mask"]),
            (pair_mask[:], w["pair_mask"]), (upper[:], w["upper"]),
            (wk[:, A:2 * A], w["qkT"][:, A:2 * A]), (wq[:, A:2 * A], w["qkT"][:, 0:A]),
            (wvs[:], w["vsT"]), (wv2[:, 0:A], w["vsT"][:, 0:A]), (wv2[:, A:C], w["vsT"][:, 0:A]),
            (projT[:], w["projT"]), (proj_y[0:A, 0, :], w["projT"][0:A, :]),
            (proj_y[A:C, 1, :], w["projT"][0:A, :]),
            (fu1T[:], w["fu1T"]), (fu2T[:], w["fu2T"]), (w1T[:], w["w1T"]), (w2T[:], w["w2T"]),
            (ln_w[:], w["ln_w"]), (ln_b[:], w["ln_b"]),
            (q_b[0:A, :], w["qk_b"][0:A, :]), (q_b[A:C, :], w["qk_b"][0:A, :]),
            (k_b[0:A, :], w["qk_b"][A:C, :]), (k_b[A:C, :], w["qk_b"][A:C, :]),
            (vs_b[:], w["vs_b"]), (v2_b[0:A, :], w["vs_b"][0:A, :]), (v2_b[A:C, :], w["vs_b"][0:A, :]),
            (depth_w[:], w["depth_w"]), (depth_b[:], w["depth_b"]), (proj_b[:], w["proj_b"]),
            (bn[:, 0:1], w["gamma"]), (bn[:, 1:2], w["beta"]), (bn[:, 2:3], w["rmean"]),
            (bn[:, 3:4], w["rvar"]), (b2[:], w["b2"][:, 0:4]), (l1_b[:], w["l1_b"]),
        ]
        N_DVE_SET = 11
        N_MID, MID_STEPS, MID_PE = 38, 8, 8
        N_ZERO = 3
        N_PAD = 10

        def chunk(ap):
            return ap.rearrange("c (r x) -> c r x", x=W)

        def rows_of(i, c):
            return i * WS + SH if c == 0 else (i * WS + WS) % H

        block = ctx.enter_context(nc.Block())

        @block.sync
        def _(sp):
            for s in stored:
                sp.sem_inc(s, FREE)
            def load_x(b, i, c):
                sp.dma_start(chunk(xc[:, c, :]), x[b, :, bass.ds(rows_of(i, c), 4), :]).then_inc(x_loaded[c], 16)

            for c in range(2):
                load_x(0, 0, c)
            sp.wait_ge(zeroed, N_ZERO)
            for dst, src in LOADS:
                sp.dma_start(dst, src).then_inc(w_loaded, 16)
            for c in range(2):
                sp.wait_ge(d_done, 1 + c)
                sp.wait_ge(xsum_done, 1 + c)
                load_x(0, 1, c)

            with sp.Fori(0, B) as b:
                with sp.Fori(0, NS) as i:
                    nxt = b * NS + i + 2
                    s = nxt % (B * NS)
                    img, strip = sp.snap(s // NS), sp.snap(s % NS)
                    for c in range(2):
                        sp.wait_ge(d_done, 2 * nxt - 1 + c)
                        sp.wait_ge(xsum_done, 2 * nxt - 1 + c)
                        load_x(img, strip, c)

                def load_x0(j, k):
                    sp.dma_start(x0[:, k, :, :], x[b, :, bass.ds(j * WS, WS), :]).then_inc(x0_loaded[k], 16)

                def store(j, k):
                    sp.wait_ge(oo_done, FREE + b * NS + j + 1)
                    sp.dma_start(out[b, :, bass.ds(j * WS, WS), :], oo[:, k, :, :]).then_inc(stored[k], 16)

                load_x0(0, 0)
                load_x0(1, 1)
                with sp.Fori(0, NS // 2 - 1) as jj:
                    for k in range(2):
                        store(2 * jj + k, k)
                        load_x0(2 * jj + 2 + k, k)
                for k in range(2):
                    store(NS - 2 + k, k)
            for k in range(2):
                sp.wait_ge(stored[k], FREE + 16 * B * NS // 2)

        @block.gpsimd
        def _(pool):
            pool.sem_inc(oo_done, FREE)
            for t in (wk, wq, proj_y):
                nc.gpsimd.memset(t[:], 0.0).then_inc(zeroed, 1)
            nc.gpsimd.memset(vsp[:], 0.0).then_inc(padded, 1)
            nc.gpsimd.memset(vd[:], 0.0).then_inc(padded, 1)
            nc.gpsimd.memset(zs[:], 0.0).then_inc(padded, 1)
            nc.gpsimd.memset(edge[:], 0.0).then_inc(padded, 1)
            nc.gpsimd.memset(eps[:, 0:1], LN_EPS).then_inc(padded, 1)
            nc.gpsimd.memset(eps[:, 1:2], BN_EPS).then_inc(padded, 1)
            pool.wait_ge(padded, 6)
            for h in range(2):
                for k in range(2):
                    nc.gpsimd.memset(vd[h * K:(h + 1) * K, k, :, :, :, h, HD], 1.0).then_inc(padded, 1)
            pool.wait_ge(padded, N_PAD)

            with pool.Fori(0, B) as b:
                with pool.Fori(0, NS // 2) as jj:
                    for k in range(2):
                        u = b * NS + 2 * jj + k
                        pool.wait_ge(ob_done, FREE + 2 * (u + 1))
                        nc.gpsimd.tensor_tensor(ob[:], ob[:], oc[:], ALU.add).then_inc(od_done, 1)
                        pool.wait_ge(od_done, u + 1)
                        pool.wait_ge(oa_done, 2 * (u + 1))
                        pool.wait_ge(stored[k], FREE + 16 * (b * (NS // 2) + jj))
                        nc.gpsimd.tensor_tensor(oo[:, k, :, :], ob[:], oa[:, k, :, :], ALU.add).then_inc(oo_done, 1)

        @block.tensor
        def _(pe):
            mm = nc.tensor.matmul

            def d_of(s, c):
                pe.wait_ge(x_loaded[c], 16 * (s + 1))
                if not (isinstance(s, int) and s == 0 and c == 0):
                    pe.wait_ge(xn_done, 4 * s + 2 * c)
                mm(ps_d, center[:], xc[:, c, :], start=True, stop=True).then_inc(d_done, 1)

            def var_of(s, c):
                pe.wait_ge(sq_done, 2 * s + c + 1)
                mm(ps_var, mean_w[:], sq[:], start=True, stop=True).then_inc(var_done, 1)

            pe.wait_ge(w_loaded, 16 * len(LOADS))
            bias_ps = banks_s[:C, 0, 0:4]
            mm(bias_ps[:, 0:1], wk[:, A:3 * A], ln_b[:], start=True, stop=False)
            mm(bias_ps[:, 0:1], wk[:, 0:2 * A], ln_b[:], start=False, stop=True).then_inc(pe_set, 1)
            mm(bias_ps[:, 1:2], wq[:, A:3 * A], ln_b[:], start=True, stop=False)
            mm(bias_ps[:, 1:2], wq[:, 0:2 * A], ln_b[:], start=False, stop=True).then_inc(pe_set, 1)
            mm(bias_ps[:, 2:3], wvs[:], ln_b[:], start=True, stop=True).then_inc(pe_set, 1)
            mm(bias_ps[:, 3:4], wv2[:], ln_b[:], start=True, stop=True).then_inc(pe_set, 1)
            def keys_queries(s, k):
                win = lambda w: xn[:, k, :, SH + w * W // 2:SH + (w + 1) * W // 2].rearrange(
                    "c r (p x) -> c p r x", x=WS)
                pe.wait_ge(xn_done, 4 * (s + 1))
                for n, wt in enumerate((wk, wq)):
                    if not (isinstance(s, int) and s == 0):
                        pe.wait_ge(vsp_done, 2 * s - 1 + n)
                    mm(banks_g[:C, n, :], wt[:, A:3 * A], win(0), start=True, stop=False)
                    mm(banks_g[:C, n, :], wt[:, 0:2 * A], win(1), start=False, stop=True).then_inc(kq_done, 1)

            def v_transposed(s):
                pe.wait_ge(xw_done, 2 * (s + 1))
                if not (isinstance(s, int) and s == 0):
                    pe.wait_ge(sd_done, 4 * s - 1)
                for p in range(NP):
                    lhs = xw[:, p, :, :].rearrange("c w k -> c (w k)")
                    last = mm(banks_s[:, 0, p * A:(p + 1) * A], lhs, wvs[:, 0:A], start=True, stop=True)
                last.then_inc(vt_done, 1)

            for c in range(2):
                d_of(0, c)
                var_of(0, c)
            pe.wait_ge(dve_set, N_DVE_SET)
            pe.wait_ge(padded, N_PAD)
            keys_queries(0, 0)
            d_of(1, 0)
            var_of(1, 0)
            v_transposed(0)
            d_of(1, 1)
            var_of(1, 1)

            def phase_a(b, i, k):
                t = b * NS + i

                def scores(q):
                    for e in range(2):
                        p = 2 * q + e
                        last = mm(banks_s[:, q % 2, e * 256:(e + 1) * 256],
                                  qd[:, p, :, :].rearrange("c w k -> c (w k)"),
                                  kd[:, p, :, :].rearrange("c h k -> c (h k)"), start=True, stop=True)
                    last.then_inc(s_done, 1)

                def transposes(q):
                    pe.wait_ge(pr_done, FREE + 4 * t + q + 1)
                    if q > 0:
                        pe.wait_ge(pt_done, 4 * t + q)
                    for j in range(4):
                        last = nc.tensor.transpose(ps_tp[:, j * 128:(j + 1) * 128],
                                                   pr[:, q % 2, j * 128:(j + 1) * 128], ident[:])
                    last.then_inc(tp_done, 1)

                def values(q):
                    pe.wait_ge(pt_done, 4 * t + q + 1)
                    bank = ps_o if q < 2 else banks_s[:, 1, :]
                    for j in range(4):
                        at = (q % 2) * 208 + j * 52
                        last = mm(bank[:, at:at + 52], pt[:, q % 2, j * 128:(j + 1) * 128],
                                  vd[:, k, 2 * q + j // 2, j % 2, :, :, :].rearrange("k w h d -> k (w h d)"),
                                  start=True, stop=True)
                    last.then_inc(pv_done, 1)

                pe.wait_ge(kd_done, 4 * (t + 1))
                pe.wait_ge(qd_done, 2 * (t + 1))
                pe.wait_ge(vd_done, 4 * (t + 1))
                pe.wait_ge(zs_done, FREE + 2 * NS * b)
                scores(0)
                scores(1)
                for c in range(2):
                    mm(banks_g[:C, c, :], wvs[:], xn[:, k, 4 * c:4 * c + 4, 0:W],
                       start=True, stop=True).then_inc(vs_done, 1)
                d_of(t + 2, 0)
                transposes(0)
                pe.wait_ge(sd_done, 4 * t + 1)
                scores(2)
                transposes(1)
                pe.wait_ge(sd_done, 4 * t + 2)
                scores(3)
                keys_queries(t + 1, 1 - k)
                pe.wait_ge(y1_done, FREE + 2 * t)
                values(0)
                values(1)
                transposes(2)
                var_of(t + 2, 0)
                v_transposed(t + 1)
                transposes(3)
                d_of(t + 2, 1)
                pe.wait_ge(sd_done, 4 * (t + 1))
                values(2)
                values(3)
                var_of(t + 2, 1)
                pe.wait_ge(yq_done, 4 * (t + 1))
                for e in range(4):
                    last = nc.tensor.transpose(ps_o[:C, e * 128:(e + 1) * 128],
                                               yq[:, e, :, :].rearrange("q g c -> q (g c)"), ident[:])
                last.then_inc(yt_done, 1)

            def between(b):
                one = banks_s[:, 0, :]
                pe.wait_ge(vd_done, 4 * (NS * (b + 1) + 1))
                pe.wait_ge(kd_done, 4 * (NS * (b + 1) + 1))
                pe.wait_ge(qd_done, 2 * (NS * (b + 1) + 1))
                for lhs, rhs, at, m, dve in (
                    (fold[:], st[:, 0:1], 0, C, 1),
                    (fu1T[:], st[:, 5:6], 1, R, 2),
                    (fu2T[:], tr[:, 1:2], 2, C, 3),
                    (spread[:], st[:, 9:10], 3, C, 4),
                    (projT[:], st[:, 12:13], 4, C, 5),
                    (projT[:], st[:, 13:14], 5, C, 5),
                    (w1T[:], st[:, 14:15], 6, R, 6),
                ):
                    pe.wait_ge(mid_to_pe, MID_STEPS * b + dve)
                    mm(one[0:m, at:at + 1], lhs, rhs, start=True, stop=True).then_inc(mid_pe, 1)
                pe.wait_ge(mid_to_pe, MID_STEPS * b + 7)
                for k in range(4):
                    last = mm(one[0:C, 8 + k:9 + k], w2T[:, k, :], tr[:, 5:6], start=True, stop=True)
                last.then_inc(mid_pe, 1)

            def conv(b, j, k, first):
                if k == 0:
                    bank = banks_g
                else:
                    bank = banks_h
                if first:
                    pe.wait_ge(mid_to_pe, MID_STEPS * (b + 1))
                else:
                    pe.wait_ge(m_step, len(DVE_TAPS) * (b * NS + j - 2) + 1)
                for c in range(2):
                    for n, tap in enumerate(PE_TAPS):
                        dh, dw = TAPS[tap]
                        last = mm(bank[:C, c, :], diag[:, n, :],
                                  vsp[:, bass.ds(j * WS + 4 * c + 1 + dh, 4), 1 + dw:1 + dw + W],
                                  start=n == 0, stop=n == len(PE_TAPS) - 1)
                last.then_inc(conv_done, 1)

            def project(b, j, k):
                u = b * NS + j
                pe.wait_ge(wrap_done, u + 1)
                pe.wait_ge(zs_done, FREE + 2 * u)
                for c in range(2):
                    z = banks_s[:C, c, :]
                    mm(z, projT[:], mb[:, k, 4 * c:4 * c + 4, SH:XW], start=True, stop=False)
                    yrow = (j * WS + H - SH) % H if c == 0 else j * WS
                    zr = chunk(z).rearrange("c r (w g x) -> c r w g x", w=2, g=2)
                    for g in range(2):
                        last = mm(zr[:, :, :, g, :], proj_yc[:, g, :], y1[:, bass.ds(yrow, 4), :, :],
                                  start=False, stop=g == 1)
                last.then_inc(z_done, 1)

            with pe.Fori(0, B) as b:
                with pe.Fori(0, NS // 2) as ii:
                    for k in range(2):
                        phase_a(b, 2 * ii + k, k)
                between(b)
                conv(b, 0, 0, True)
                conv(b, 1, 1, True)
                project(b, 0, 0)
                with pe.Fori(0, NS // 2 - 1) as jj:
                    conv(b, 2 * jj + 2, 0, False)
                    project(b, 2 * jj + 1, 1)
                    conv(b, 2 * jj + 3, 1, False)
                    project(b, 2 * jj + 2, 0)
                project(b, NS - 1, 1)

        @block.scalar
        def _(act):
            for s in (pr_done, y1_done, ob_done):
                act.sem_inc(s, FREE)
            fn = nc.scalar.activation
            act.preload_act_table_set("natural_log_exp_and_others")

            def square(s, c):
                act.wait_ge(d_done, 2 * s + c + 1)
                fn(sq[:], ps_d, ACT.Square).then_inc(sq_done, 1)

            def rsqrt(s, c):
                act.wait_ge(var_done, 2 * s + c + 1)
                fn(lnv[:], ps_var, ACT.Ln, bias=eps[:, 0:1]).then_inc(ln_done, 1)
                act.wait_ge(ln_done, 2 * s + c + 1)
                fn(rstd[:], lnv[:], ACT.Exp, scale=-0.5).then_inc(rstd_done, 1)

            act.wait_ge(padded, N_PAD)
            for c in range(2):
                square(0, c)
                rsqrt(0, c)
            act.wait_ge(w_loaded, 16 * len(LOADS))
            fn(bn_scale[:], bn[:, 3:4], ACT.Ln, bias=eps[:R, 1:2]).then_inc(act_set, 1)
            act.wait_ge(act_set, 1)
            fn(bn_scale[:], bn_scale[:], ACT.Exp, scale=-0.5).then_inc(act_set, 1)
            act.wait_ge(dve_set, N_DVE_SET)

            def keys(s):
                act.wait_ge(kq_done, 2 * s + 1)
                for h in range(HEADS):
                    fn(kd[:, :, h, :], banks_g[:C, 0, :].rearrange("c (p k) -> c p k", k=K), ACT.Identity,
                       bias=k_bias[:, h:h + 1], scale=head_mask[:, h:h + 1]).then_inc(kd_done, 1)

            def values(s, k):
                act.wait_ge(vt_done, s + 1)
                for wi in range(2):
                    for h in range(2):
                        src = banks_s[wi * K:(wi + 1) * K, 0, 0:NP * A].rearrange(
                            "k (p s h d) -> k p s h d", s=2, h=2, d=HD)
                        fn(vd[h * K:(h + 1) * K, k, :, :, wi, h, 0:HD], src[:, :, :, h, :], ACT.Copy).then_inc(vd_done, 1)

            keys(0)
            square(1, 0)
            rsqrt(1, 0)
            values(0, 0)
            square(1, 1)
            rsqrt(1, 1)

            def phase_a(b, i, k):
                t = b * NS + i

                def exps(q):
                    act.wait_ge(sd_done, 4 * t + q + 1)
                    fn(pr[:, q % 2, :], sd[:, q % 2, :], ACT.Exp).then_inc(pr_done, 1)

                def transposed(q):
                    act.wait_ge(tp_done, 4 * t + q + 1)
                    fn(pt[:, q % 2, :], ps_tp[:, :], ACT.Copy).then_inc(pt_done, 1)

                def vs_out(c):
                    act.wait_ge(vs_done, 2 * t + c + 1)
                    fn(vsp[:, bass.ds(rows_of(i, c) + 1, 4), 1:1 + W], chunk(banks_g[:C, c, :]), ACT.Identity,
                       bias=vs_bias[:], accum_out=vstat[:, bass.ds(2 * i + c, 1)]).then_inc(vsp_done, 1)

                exps(0)
                vs_out(0)
                exps(1)
                vs_out(1)
                square(t + 2, 0)
                transposed(0)
                exps(2)
                transposed(1)
                exps(3)
                keys(t + 1)
                transposed(2)
                rsqrt(t + 2, 0)
                values(t + 1, 1 - k)
                transposed(3)
                square(t + 2, 1)
                rsqrt(t + 2, 1)
                act.wait_ge(yt_done, t + 1)
                src = ps_o[:C, :].rearrange("c (e w r x) -> c e w r x", e=4, w=2, x=WS)
                for wi in range(2):
                    dst = y1[:, bass.ds(i * WS, WS), wi, :].rearrange("c r (e x) -> c e r x", x=WS)
                    fn(dst, src[:, :, wi, :, :], ACT.Identity, bias=y_bias[:],
                       accum_out=ystat[:, bass.ds(2 * i + wi, 1)]).then_inc(y1_done, 1)

            def phase_b(b, j, k):
                u = b * NS + j
                act.wait_ge(m_step, len(DVE_TAPS) * (u + 1))
                fn(mb[:, k, :, W:XW], mb[:, k, :, 0:SH], ACT.Copy).then_inc(wrap_done, 1)

            def taps(b, j, k):
                u = b * NS + j
                act.wait_ge(zs_done, FREE + 2 * (u + 1))
                act.wait_ge(oo_done, FREE + u)
                for n, (o, tap) in enumerate(((ob, 2), (oc, 3))):
                    dh, dw = L1_TAPS[tap]
                    fn(o[:], zs[:, k, 1 + dh:1 + dh + WS, 1 + dw:1 + dw + W], ACT.Copy,
                       scale=l1_w[:, tap:tap + 1]).then_inc(ob_done, 1)

            with act.Fori(0, B) as b:
                with act.Fori(0, NS // 2) as ii:
                    for k in range(2):
                        phase_a(b, 2 * ii + k, k)
                act.wait_ge(mid_pe, MID_PE * b + 3)
                fn(st[:, 6:7], banks_s[:C, 0, 2:3], ACT.Exp, scale=-1.0).then_inc(mid_act, 1)
                phase_b(b, 0, 0)
                with act.Fori(0, NS // 2 - 1) as jj:
                    phase_b(b, 2 * jj + 1, 1)
                    taps(b, 2 * jj, 0)
                    phase_b(b, 2 * jj + 2, 0)
                    taps(b, 2 * jj + 1, 1)
                phase_b(b, NS - 1, 1)
                taps(b, NS - 2, 0)
                taps(b, NS - 1, 1)

        @block.vector
        def _(dve):
            dve.sem_inc(zs_done, FREE)
            v = nc.vector

            def sum_x(s, c):
                dve.wait_ge(x_loaded[c], 16 * (s + 1))
                v.tensor_reduce(xstat[:, bass.ds(2 * s + c, 1)], xc[:, c, :], AX.X, ALU.add).then_inc(xsum_done, 1)

            def normalise(s, c, k):
                dve.wait_ge(rstd_done, 2 * s + c + 1)
                d, r = chunk(ps_d), chunk(rstd[:])
                rows = xn[:, k, 4 * c:4 * c + 4, :]
                v.tensor_tensor(rows[:, :, 0:W], d, r, ALU.mult).then_inc(xn_done, 1)
                v.tensor_tensor(rows[:, :, W:XW], d[:, :, 0:SH], r[:, :, 0:SH], ALU.mult).then_inc(xn_done, 1)

            def by_windows(s, k):
                dve.wait_ge(xn_done, 4 * (s + 1))
                if not (isinstance(s, int) and s == 0):
                    dve.wait_ge(vt_done, s)
                for wi in range(2):
                    px = xn[:, k, :, SH + wi * W // 2:SH + (wi + 1) * W // 2]
                    v.tensor_copy(xw[:, :, wi, :].rearrange("c p (r x) -> c p r x", x=WS),
                                  px.rearrange("c r (p x) -> c p r x", x=WS)).then_inc(xw_done, 1)

            def queries(s):
                dve.wait_ge(kq_done, 2 * s + 2)
                for wi in range(2):
                    v.tensor_scalar(qd[:, :, wi, :], banks_g[:C, 1, :].rearrange("c (p k) -> c p k", k=K),
                                    q_scale[:, wi:wi + 1], q_bias[:, wi:wi + 1], ALU.mult, ALU.add).then_inc(qd_done, 1)

            for c in range(2):
                sum_x(0, c)
                normalise(0, c, 0)
            by_windows(0, 0)
            dve.wait_ge(pe_set, 4)
            bias_ps = banks_s[:C, 0, 0:4]
            n = [0]

            def setup(ins):
                ins.then_inc(dve_set, 1)
                n[0] += 1
                dve.wait_ge(dve_set, n[0])

            dve.wait_ge(w_loaded, 16 * len(LOADS))
            for t, width in ((wk, 3 * A), (wq, 3 * A), (wvs, C)):
                setup(v.tensor_scalar(t[:], t[:], ln_w[:], None, ALU.mult))
            setup(v.tensor_tensor(k_b[:], bias_ps[:, 0:1], k_b[:], ALU.add))
            setup(v.tensor_tensor(q_b[:], bias_ps[:, 1:2], q_b[:], ALU.add))
            setup(v.tensor_tensor(vs_bias[:], bias_ps[:, 2:3], vs_b[:], ALU.add))
            setup(v.tensor_tensor(y_bias[:], bias_ps[:, 3:4], v2_b[:], ALU.add))
            setup(v.tensor_scalar(k_bias[:], head_mask[:], k_b[:], None, ALU.mult))
            setup(v.tensor_scalar(q_bias[:], pair_mask[:], q_b[:], SCALE, ALU.mult, ALU.mult))
            setup(v.tensor_scalar(q_scale[:], pair_mask[:], SCALE, None, ALU.mult))
            dve.wait_ge(act_set, 2)
            setup(v.tensor_tensor(bn_scale[:], bn_scale[:], bn[:, 0:1], ALU.mult))
            assert n[0] == N_DVE_SET

            queries(0)
            for c in range(2):
                sum_x(1, c)
                normalise(1, c, 1)
            by_windows(1, 1)

            def phase_a(b, i, k):
                t = b * NS + i

                def softmax(q):
                    dve.wait_ge(s_done, 4 * t + q + 1)
                    s = banks_s[:, q % 2, :].rearrange("p (g k) -> p g k", k=K)
                    v.tensor_reduce(mx[:, q, :], s, AX.X, ALU.max).then_inc(mx_done, 1)
                    dve.wait_ge(mx_done, 4 * t + q + 1)
                    if q < 2:
                        dve.wait_ge(pr_done, FREE + 4 * t)
                    else:
                        dve.wait_ge(pr_done, FREE + 4 * t + q - 1)
                    v.tensor_tensor(sd[:, q % 2, :].rearrange("p (g k) -> p g k", k=K), s,
                                    mx[:, q, :].unsqueeze(2).to_broadcast([128, 8, K]),
                                    ALU.subtract).then_inc(sd_done, 1)

                def divide(half):
                    dve.wait_ge(pv_done, 4 * t + 2 * half + 2)
                    bank = ps_o if half == 0 else banks_s[:, 1, :]
                    o = bank[:, 0:416].rearrange("q (n w h d) -> q n w h d", w=2, h=2, d=VW)
                    for wi in range(2):
                        r = slice(wi * K, (wi + 1) * K)
                        rc = rec[r, half, :].rearrange("q (n h) -> q n h", h=2)
                        v.reciprocal(rc, o[r, :, wi, :, HD]).then_inc(rec_done, 1)
                    for wi in range(2):
                        dve.wait_ge(rec_done, 4 * t + 2 * half + wi + 1)
                        r = slice(wi * K, (wi + 1) * K)
                        rc = rec[r, half, :].rearrange("q (n h) -> q n h", h=2)
                        v.tensor_tensor(yq[r, :, half, :].rearrange("q e (s h d) -> q e s h d", s=2, d=HD),
                                        o[r, :, wi, :, 0:HD].rearrange("q (e s) h d -> q e s h d", s=2), rc.rearrange("q (e s) h -> q e s h", s=2).unsqueeze(4).to_broadcast([K, 4, 2, 2, HD]),
                                        ALU.mult).then_inc(yq_done, 1)

                softmax(0)
                softmax(1)
                sum_x(t + 2, 0)
                softmax(2)
                sum_x(t + 2, 1)
                softmax(3)
                queries(t + 1)
                divide(0)
                normalise(t + 2, 0, k)
                divide(1)
                normalise(t + 2, 1, k)
                by_windows(t + 2, k)

            def between(b):
                n = [0]

                def step(ins):
                    ins.then_inc(mid_dve, 1)
                    n[0] += 1
                    dve.wait_ge(mid_dve, N_MID * b + n[0])

                def to_pe(ins):
                    ins.then_inc(mid_to_pe, 1)
                    k[0] += 1
                    dve.wait_ge(mid_to_pe, MID_STEPS * b + k[0])

                k = [0]
                one = banks_s[:, 0, :]
                s = lambda i, w=1: st[:, i:i + w]
                img = vsp[:, 1:1 + H, 1:1 + W]
                dve.wait_ge(ob_done, FREE + 2 * NS * b)
                dve.wait_ge(y1_done, FREE + 2 * NS * (b + 1))
                dve.wait_ge(vsp_done, 2 * NS * (b + 1))
                dve.wait_ge(xsum_done, 2 * NS * (b + 1))
                to_pe(v.tensor_reduce(s(0), ystat[:], AX.X, ALU.add))
                step(v.tensor_reduce(s(1), vstat[:], AX.X, ALU.add))
                step(v.tensor_reduce(s(2), xstat[:, bass.ds(2 * NS * b, 2 * NS)], AX.X, ALU.add))
                for at, rows in ((0, H - 1), (2, 0)):
                    step(v.tensor_reduce(edge[:, at:at + 1], img[:, rows, :], AX.X, ALU.add))
                    step(v.tensor_reduce(edge[:, 3 + at:4 + at], img[:, :, rows], AX.X, ALU.add))
                    for bt, cols in ((0, W - 1), (2, 0)):
                        step(v.tensor_copy(edge[:, 6 + 3 * at + bt:7 + 3 * at + bt], img[:, rows, cols:cols + 1]))
                e3 = edge[:, 6:15].rearrange("c (a b) -> c a b", b=3)
                sums = edge[:, 15:24].rearrange("c (a b) -> c a b", b=3)
                step(v.tensor_tensor(sums, e3, edge[:, 0:3].unsqueeze(2).to_broadcast([C, 3, 3]), ALU.subtract))
                step(v.tensor_tensor(sums, sums, edge[:, 3:6].unsqueeze(1).to_broadcast([C, 3, 3]), ALU.subtract))
                step(v.tensor_scalar(edge[:, 15:24], edge[:, 15:24], s(1), 1.0 / PX, ALU.add, ALU.mult))
                step(v.tensor_tensor(edge[:, 15:24], edge[:, 15:24], depth_w[:], ALU.mult))
                step(v.tensor_reduce(s(3), edge[:, 15:24], AX.X, ALU.add))
                step(v.tensor_tensor(s(3), s(3), depth_b[:], ALU.add))
                step(v.tensor_tensor(s(4), s(1), upper[:], ALU.mult))
                dve.wait_ge(mid_pe, MID_PE * b + 1)
                step(v.tensor_tensor(s(4), one[:C, 0:1], s(4), ALU.add))
                step(v.tensor_scalar(s(4), s(4), 1.0 / PX, None, ALU.mult))
                to_pe(v.tensor_tensor(s(5), s(4), s(3), ALU.add))
                dve.wait_ge(mid_pe, MID_PE * b + 2)
                step(v.tensor_scalar(tr[:, 0:1], one[:R, 1:2], 0.2, None, ALU.mult))
                to_pe(v.tensor_tensor(tr[:, 1:2], one[:R, 1:2], tr[:, 0:1], ALU.max))
                dve.wait_ge(mid_act, b + 1)
                step(v.tensor_scalar(s(7), s(6), 1.0, None, ALU.add))
                to_pe(v.reciprocal(s(9), s(7)))
                step(v.tensor_scalar(s(10), s(9), -1.0, 1.0, ALU.mult, ALU.add))
                step(v.tensor_tensor(s(11), s(4), s(9), ALU.mult))
                step(v.scalar_tensor_tensor(out=s(12), in0=s(3), scalar=s(10), in1=s(11), op0=ALU.mult, op1=ALU.add))
                to_pe(v.tensor_tensor(s(13), depth_b[:], s(10), ALU.mult))
                dve.wait_ge(mid_pe, MID_PE * b + 6)
                step(v.tensor_tensor(s(15), one[:C, 4:5], proj_b[:], ALU.add))
                to_pe(v.scalar_tensor_tensor(out=s(14), in0=s(2), scalar=1.0 / PX, in1=s(15), op0=ALU.mult, op1=ALU.add))
                dve.wait_ge(mid_pe, MID_PE * b + 7)
                step(v.tensor_copy(s(17), one[:C, 3:4]))
                step(v.tensor_tensor(z_bias[:], one[:C, 5:6], proj_b[:], ALU.add))
                step(v.tensor_tensor(tr[:, 3:4], one[:R, 6:7], bn[:, 2:3], ALU.subtract))
                step(v.scalar_tensor_tensor(out=tr[:, 4:5], in0=tr[:, 3:4], scalar=bn_scale[:], in1=bn[:, 1:2],
                                            op0=ALU.mult, op1=ALU.add))
                to_pe(v.tensor_scalar(tr[:, 5:6], tr[:, 4:5], 0.0, None, ALU.max))
                step(v.tensor_scalar(tap_w[:], depth_w[:], s(10), None, ALU.mult))
                step(v.tensor_tensor(s(16), s(9), upper[:], ALU.mult))
                step(v.tensor_tensor(tap_w[:, 4:5], tap_w[:, 4:5], s(16), ALU.add))
                step(v.tensor_scalar(proj_yc[:].rearrange("c g o -> c (g o)"), proj_y[:].rearrange("c g o -> c (g o)"),
                                     s(17), None, ALU.mult))
                for m, tap in enumerate(PE_TAPS):
                    step(v.tensor_scalar(diag[:, m, :], ident[:C, :C], tap_w[:, tap:tap + 1], None, ALU.mult))
                step(v.memset(zs[:, 1, WS, :], 0.0))
                dve.wait_ge(mid_pe, MID_PE * (b + 1))
                to_pe(v.tensor_tensor(l1_w[:], one[:C, 8:12], b2[:], ALU.add))
                assert (n[0], k[0]) == (N_MID, MID_STEPS), (n[0], k[0])

            def mix(b, j, k):
                u = b * NS + j
                bank = banks_g if k == 0 else banks_h
                dve.wait_ge(conv_done, u + 1)
                for n, tap in enumerate(DVE_TAPS):
                    dh, dw = TAPS[tap]
                    acc = mb[:, k, :, 0:W]
                    if n:
                        dve.wait_ge(m_step, len(DVE_TAPS) * u + n)
                    src = bank[:C, :, :].rearrange("c a (r x) -> c (a r) x", x=W) if n == 0 else acc
                    v.scalar_tensor_tensor(out=acc, in0=vsp[:, bass.ds(j * WS + 1 + dh, WS), 1 + dw:1 + dw + W],
                                           scalar=tap_w[:, tap:tap + 1], in1=src,
                                           op0=ALU.mult, op1=ALU.add).then_inc(m_step, 1)

            def residual(b, j, jj, k):
                u = b * NS + j
                dve.wait_ge(z_done, u + 1)
                dve.wait_ge(x0_loaded[k], 16 * (b * (NS // 2) + jj + 1))
                v.tensor_copy(zs[:, k, 0, :], zs[:, 1 - k, WS, :]).then_inc(halo_done, 1)
                z = banks_s[:C, :, :].rearrange("c a (r x) -> c (a r) x", x=W)
                v.scalar_tensor_tensor(out=zs[:, k, 1:1 + WS, 1 + SH:1 + W], in0=z[:, :, 0:W - SH], scalar=z_bias[:],
                                       in1=x0[:, k, :, SH:W], op0=ALU.add, op1=ALU.add).then_inc(zs_done, 1)
                v.scalar_tensor_tensor(out=zs[:, k, 1:1 + WS, 1:1 + SH], in0=z[:, :, W - SH:W], scalar=z_bias[:],
                                       in1=x0[:, k, :, 0:SH], op0=ALU.add, op1=ALU.add).then_inc(zs_done, 1)

            def taps(b, j, k):
                u = b * NS + j
                dve.wait_ge(zs_done, FREE + 2 * (u + 1))
                dve.wait_ge(halo_done, u + 1)
                for n in range(2):
                    dh, dw = L1_TAPS[n]
                    src = zs[:, k, 1 + dh:1 + dh + WS, 1 + dw:1 + dw + W]
                    if n == 0:
                        ins = v.tensor_scalar(oa[:, k, :, :], src, l1_w[:, 0:1], l1_b[:], ALU.mult, ALU.add)
                    else:
                        dve.wait_ge(oa_done, 2 * u + 1)
                        ins = v.scalar_tensor_tensor(out=oa[:, k, :, :], in0=src, scalar=l1_w[:, 1:2],
                                                     in1=oa[:, k, :, :], op0=ALU.mult, op1=ALU.add)
                    ins.then_inc(oa_done, 1)

            def finish(b, j, jj, k):
                u = b * NS + j
                ago = NS * b if isinstance(j, int) and j == 0 else u - 1
                dve.wait_ge(ob_done, FREE + 2 * ago)
                dve.wait_ge(oo_done, FREE + ago)
                residual(b, j, jj, k)
                taps(b, j, k)

            with dve.Fori(0, B) as b:
                with dve.Fori(0, NS // 2) as ii:
                    for k in range(2):
                        phase_a(b, 2 * ii + k, k)
                between(b)
                mix(b, 0, 0)
                mix(b, 1, 1)
                finish(b, 0, 0, 0)
                with dve.Fori(0, NS // 2 - 1) as jj:
                    mix(b, 2 * jj + 2, 0)
                    finish(b, 2 * jj + 1, jj, 1)
                    mix(b, 2 * jj + 3, 1)
                    finish(b, 2 * jj + 2, jj + 1, 0)
                finish(b, NS - 1, NS // 2 - 1, 1)


def kernel(**inputs):
    import concourse.bacc as bacc
    from concourse.bass_utils import run_bass_kernel_spmd

    arr = {k: np.asarray(v) for k, v in inputs.items()}
    l0 = {k[len("L0_conv_"):]: v for k, v in arr.items() if k.startswith("L0_conv_")}
    l1 = {k[len("L1_conv_"):]: v for k, v in arr.items() if k.startswith("L1_conv_")}
    col = lambda a: a.reshape(-1, 1)
    row = np.arange(C)
    w = {
        "center": np.eye(C) - 1.0 / C,
        "mean_w": np.full((C, C), 1.0 / C),
        "ident": np.eye(128),
        "fold": row[:, None] % A == row[None, :],
        "spread": row[:, None] == row[None, :] % A,
        "head_mask": (row[:, None] % A) // HD == np.arange(HEADS)[None, :],
        "pair_mask": row[:, None] // A == np.arange(2)[None, :],
        "upper": row[:, None] >= A,
    }
    w = {k: v.astype(np.float32) for k, v in w.items()}
    w |= {
        "qkT": l0["qk_w"].T, "vsT": l0["vs_w"].T, "projT": l0["proj_w"].T,
        "fu1T": l0["fu1_w"].T, "fu2T": l0["fu2_w"].T, "w1T": l1["w1"].T,
        "w2T": l1["w2"].reshape(C, 9, R)[:, 0:4].transpose(2, 1, 0),
        "ln_w": col(l0["ln_w"]), "ln_b": col(l0["ln_b"]), "qk_b": col(l0["qk_b"]), "vs_b": col(l0["vs_b"]),
        "depth_w": l0["depth_w"].reshape(C, 9), "depth_b": col(l0["depth_b"]), "proj_b": col(l0["proj_b"]),
        "gamma": col(l1["gamma"]), "beta": col(l1["beta"]), "rmean": col(l1["running_mean"]),
        "rvar": col(l1["running_var"]), "b2": l1["b2"].reshape(C, 9), "l1_b": col(l1["bias"]),
    }
    arrays = {"in_x": arr["x"].reshape(B, C, H, W)} | {f"in_{k}": v for k, v in w.items()}
    arrays = {k: np.ascontiguousarray(v) for k, v in arrays.items()}

    nc = bacc.Bacc("TRN2", target_bir_lowering=False, num_devices=1)
    dram = {k: nc.dram_tensor(k, v.shape, F32, kind="ExternalInput").ap() for k, v in arrays.items()}
    out = nc.dram_tensor("out_0", (B, C, H, W), F32, kind="ExternalOutput").ap()
    program(nc, dram["in_x"], out, {k[3:]: v for k, v in dram.items()})
    return run_bass_kernel_spmd(nc, [arrays], core_ids=[0]).results[0]["out_0"]
```

```python
import numpy as np
import concourse.bass as bass
from concourse import mybir
from contextlib import ExitStack

F32 = mybir.dt.float32
ACT = mybir.ActivationFunctionType
ALU = mybir.AluOpType
AX = mybir.AxisListType

B, C, H, W = 4, 96, 128, 128
WS, HEADS = 8, 4
SH = WS // 2
A = C // 2
SECOND = 64
QK = SECOND + A
HD = A // HEADS
SCALE = HD ** -0.5
LN_EPS, BN_EPS = 1e-6, 1e-5
R = C // 4
NS = H // WS
NP = W // WS // 2
K = WS * WS
CH = 4 * W
PX = H * W
XW = W + SH
VW = HD + 1
TAPS = [(k // 3 - 1, k % 3 - 1) for k in range(9)]
PE_TAPS = ((4, 0, 2), (4, 0))
ACT_TAP = 1
DVE_TAPS = tuple([k for k in range(9) if k not in pe and k != ACT_TAP] for pe in PE_TAPS)
MIX = [(1, DVE_TAPS[1][0])] + [step for n in range(len(DVE_TAPS[0]))
                               for step in ((0, DVE_TAPS[0][n]), (1, DVE_TAPS[1][n + 1]))]
LN_PACK = (("center", C), ("mean_w", C))
C_PACK = (("wqk", QK), ("wvs", C), ("ln_w", 1), ("ln_b", 1), ("vs_b", 1),
          ("fold", C), ("spread", C), ("upper", 1), ("projT", C), ("proj_y", 2 * C),
          ("fu1T", R), ("w1T", R), ("depth_w", 9), ("depth_b", 1), ("proj_b", 1), ("b2", 4), ("l1_b", 1))
QK_PACK = (("head_mask", HEADS), ("qk_b", 1))
R_PACK = (("fu2T", C), ("w2T", 4 * C), ("bn", 4))
PACKS = {"ln_pack": (C, LN_PACK), "c_pack": (C, C_PACK), "qk_pack": (QK, QK_PACK), "r_pack": (R, R_PACK)}
FREE = 1
NT = NS - 1
EARLY = 2
FILL = [range(0, 1), range(1, 3), range(3, 5), range(5, 5), range(5, 7), range(7, 9), range(9, len(MIX))]
L1_TAPS = TAPS[:4]
TAP_ORDER = [1, 2, 0, 3]


def program(nc, x, out, w):
    ctx = ExitStack()
    with ctx:
        def sb(name, shape):
            return ctx.enter_context(nc.sbuf_tensor(name, shape, F32))

        def sem(name):
            return ctx.enter_context(nc.semaphore(name))

        ident = sb("ident", [128, 128])
        pack, field = {}, {}
        for name, (rows, columns) in PACKS.items():
            pack[name] = sb(name, [rows, sum(n for _, n in columns)])
            at = 0
            for what, n in columns:
                field[what] = pack[name][:, at:at + n]
                at += n
        center, mean_w = field["center"], field["mean_w"]
        head_mask = field["head_mask"]
        qk_b, wqk = field["qk_b"], field["wqk"]
        wvs, projT, vs_b = field["wvs"], field["projT"], field["vs_b"]
        ln_w, ln_b = field["ln_w"], field["ln_b"]
        fold, spread = field["fold"], field["spread"]
        upper = field["upper"]
        proj_y = field["proj_y"]
        proj_yc = sb("proj_yc", [C, 2, C])
        fu1T, fu2T, w1T = field["fu1T"], field["fu2T"], field["w1T"]
        w2T = field["w2T"].rearrange("r (k c) -> r k c", k=4)
        depth_w, depth_b, proj_b = field["depth_w"], field["depth_b"], field["proj_b"]
        b2, l1_b = field["b2"], field["l1_b"]
        bn = field["bn"]
        eps = sb("eps", [C, 2])
        k_bias = sb("k_bias", [QK, HEADS])
        vs_bias = sb("vs_bias", [C, 1])
        bn_scale = sb("bn_scale", [R, 1])

        xc = sb("xc", [C, 2, CH])
        sq = sb("sq", [C, CH])
        lnv = sb("lnv", [C, CH])
        rstd = sb("rstd", [C, CH])
        xn = sb("xn", [C, WS, XW])
        vw = sb("vw", [C, NP, 2, K])
        kd = sb("kd", [QK, NP, HEADS, K])
        qd = sb("qd", [QK, NP, 2, K])
        vd = sb("vd", [128, 2, NP, 2, 2, 2, VW])
        sd = sb("sd", [128, 2, 512])
        pr = sb("pr", [128, 2, 512])
        mx = sb("mx", [128, 4, 8])
        idle = sb("idle", [C, 1])
        rec = sb("rec", [128, 2, 16])
        yq = sb("yq", [128, 4, 2, A])
        vsp = sb("vsp", [C, H + 2, W + 2])
        y1 = sb("y1", [C, H, 2, 4 * WS])
        vstat = sb("vstat", [C, 2 * (B * NS + 2)])
        ystat = sb("ystat", [C, 2 * NS])
        xstat = sb("xstat", [C, 2 * (B * NS + 2)])

        edge = sb("edge", [C, 24])
        st = sb("st", [C, 32])
        tr = sb("tr", [R, 8])
        tap_w = sb("tap_w", [C, 9])
        l1_w = sb("l1_w", [C, 4])
        z_bias = sb("z_bias", [C, 1])
        proj_m = sb("proj_m", [C, C])
        proj_t = sb("proj_t", [C, 3, C])

        x0 = sb("x0", [C, 2, WS, W])
        mixed = sb("mixed", [128, 2, WS, W])
        mb = mixed[:C, :, :, :]
        room = mixed[:].rearrange("p k r x -> p (k r x)")
        pt = room[:, 0:2048].rearrange("p (k n) -> p k n", k=4)
        zs = sb("zs", [C, 2, WS + 1, W + 2])
        tap_out = sb("tap_out", [C, 4, WS, W])
        oo = sb("oo", [C, 2, WS, W])

        banks_ln = ctx.enter_context(nc.psum_tensor("banks_ln", [128, 2, 512], F32))
        banks_g = ctx.enter_context(nc.psum_tensor("banks_g", [128, 2, 512], F32))
        banks_s = ctx.enter_context(nc.psum_tensor("banks_s", [128, 2, 512], F32))
        banks_h = ctx.enter_context(nc.psum_tensor("banks_h", [128, 2, 512], F32))
        ps_d, ps_var = banks_ln[:C, 0, :], banks_ln[:C, 1, :]
        one = banks_ln[:, 1, :]
        ps_tp = banks_h[:, 0, :]
        ps_o = banks_h[:, 1, :]

        w_loaded = sem("w_loaded")
        ln_loaded = sem("ln_loaded")
        eps_set = sem("eps_set")
        padded = sem("padded")
        x_loaded = [sem("x_loaded0"), sem("x_loaded1")]
        x0_loaded = [sem("x0_loaded0"), sem("x0_loaded1")]
        stored = [sem("stored0"), sem("stored1")]
        pe_set = sem("pe_set")
        act_set = sem("act_set")
        dve_set = sem("dve_set")
        d_done = sem("d_done")
        sq_done = sem("sq_done")
        var_done = sem("var_done")
        ln_done = sem("ln_done")
        rstd_done = sem("rstd_done")
        xn_done = sem("xn_done")
        xsum_done = sem("xsum_done")
        kq_done = sem("kq_done")
        vt_done = sem("vt_done")
        vs_done = sem("vs_done")
        kd_done = sem("kd_done")
        kd_dve_done = sem("kd_dve_done")
        qd_done = sem("qd_done")
        vd_done = sem("vd_done")
        vw_done = sem("vw_done")
        vsp_free = sem("vsp_free")
        vsp_done = sem("vsp_done")
        s_done = sem("s_done")
        mx_done = sem("mx_done")
        sd_done = sem("sd_done")
        pr_done = sem("pr_done")
        tp_done = sem("tp_done")
        pt_done = sem("pt_done")
        pv_done = sem("pv_done")
        rec_done = sem("rec_done")
        yq_done = sem("yq_done")
        yt_done = sem("yt_done")
        y1_done = sem("y1_done")
        mid_to_pe = sem("mid_to_pe")
        mid_dve = sem("mid_dve")
        mid_pe = sem("mid_pe")
        mid_act = sem("mid_act")
        first_done = sem("first_done")
        m_step = sem("m_step")
        z_done = sem("z_done")
        halo_done = sem("halo_done")
        zs_done = sem("zs_done")
        tap_done = sem("tap_done")
        sum_done = sem("sum_done")
        oo_done = sem("oo_done")
        last_step = sem("last_step")

        N_DVE_SET = 6
        N_MID, MID_STEPS, MID_PE = 37, 8, 8
        LAST_STEPS = 9
        W_LOADS = 4
        N_ZERO = 10
        N_PAD = N_ZERO + 4

        def chunk(ap):
            return ap.rearrange("c (r x) -> c r x", x=W)

        def d_bank(s, c):
            return banks_s[:C, 1, :] if isinstance(s, int) and c == 1 else ps_d

        def rows_of(i, c):
            return i * WS + SH if c == 0 else (i * WS + WS) % H

        block = ctx.enter_context(nc.Block())

        @block.sync
        def _(sp):
            for s in stored:
                sp.sem_inc(s, FREE)
            def load_x(b, i, c):
                sp.dma_start(chunk(xc[:, c, :]), x[b, :, bass.ds(rows_of(i, c), 4), :]).then_inc(x_loaded[c], 16)

            sp.dma_start(pack["ln_pack"][:], w["ln_pack"]).then_inc(ln_loaded, 16)
            for c in range(2):
                load_x(0, 0, c)
            for name in ("c_pack", "qk_pack", "r_pack"):
                sp.dma_start(pack[name][:], w[name]).then_inc(w_loaded, 16)
            sp.dma_start(ident[:], w["ident"]).then_inc(w_loaded, 16)
            for s in (1, 2):
                for c in range(2):
                    sp.wait_ge(d_done, 2 * s - 1 + c)
                    sp.wait_ge(xsum_done, 2 * s - 1 + c)
                    load_x(0, s, c)

            with sp.Fori(0, B) as b:
                with sp.Fori(0, NS) as i:
                    nxt = b * NS + i + 3
                    s = nxt % (B * NS)
                    img, strip = sp.snap(s // NS), sp.snap(s % NS)
                    for c in range(2):
                        sp.wait_ge(d_done, 2 * nxt - 1 + c)
                        sp.wait_ge(xsum_done, 2 * nxt - 1 + c)
                        load_x(img, strip, c)

                def load_x0(j, k):
                    sp.dma_start(x0[:, k, :, :], x[b, :, bass.ds(j * WS, WS), :]).then_inc(x0_loaded[k], 16)

                def store(j, k):
                    if isinstance(j, int) and j == NS - 1:
                        src = x0
                        sp.wait_ge(last_step, LAST_STEPS * (b + 1))
                    else:
                        src = oo
                        sp.wait_ge(oo_done, FREE + b * NT + j + 1)
                    sp.dma_start(out[b, :, bass.ds(j * WS, WS), :], src[:, k, :, :]).then_inc(stored[k], 16)

                sp.wait_ge(stored[1], FREE + 16 * b * (NS // 2))
                load_x0(0, 0)
                load_x0(1, 1)
                with sp.Fori(0, NS // 2 - 1) as jj:
                    for k in range(2):
                        sp.wait_ge(zs_done, FREE + b * NS + 2 * jj + k + 1)
                        load_x0(2 * jj + 2 + k, k)
                        store(2 * jj + k, k)
                for k in range(2):
                    store(NS - 2 + k, k)
            for k in range(2):
                sp.wait_ge(stored[k], FREE + 16 * B * NS // 2)

        @block.gpsimd
        def _(pool):
            pool.sem_inc(oo_done, FREE)
            pool.sem_inc(sum_done, 2)
            for at, value in ((0, LN_EPS), (1, BN_EPS)):
                nc.gpsimd.memset(eps[:, at:at + 1], value).then_inc(eps_set, 1)
            border = [vsp[:, 0, :], vsp[:, H + 1, :], vsp[:, 1:H + 1, 0], vsp[:, 1:H + 1, W + 1]]
            for t in border + [kd[:], qd[:], vd[:], edge[:], idle[:], zs[:]]:
                nc.gpsimd.memset(t, 0.0).then_inc(padded, 1)
            pool.wait_ge(padded, N_ZERO)
            for h in range(2):
                for k in range(2):
                    nc.gpsimd.memset(vd[h * K:(h + 1) * K, k, :, :, :, h, HD], 1.0).then_inc(padded, 1)
            pool.wait_ge(padded, N_PAD)

            def to_image(b, i):
                t = b * NS + i
                pool.wait_ge(vw_done, 2 * (t + 1))
                if isinstance(i, int) and i == 0 and not (isinstance(b, int) and b == 0):
                    pool.wait_ge(zs_done, FREE + NS * (b - 1) + 2)
                nc.gpsimd.tensor_tensor(idle[:], idle[:], idle[:], ALU.add).then_inc(vsp_free, 1)
                for c in range(2):
                    rows = vsp[:, bass.ds(rows_of(i, c) + 1, 4), :]
                    strip = vw[:, :, :, 4 * WS * c:4 * WS * (c + 1)].rearrange("c p w (r x) -> c w p r x", x=WS)
                    def put(dst, src):
                        nc.gpsimd.tensor_copy(dst.rearrange("c r (p x) -> c p r x", x=min(WS, src.shape[-1])),
                                              src).then_inc(vsp_done, 1)
                    put(rows[:, :, 1 + SH:1 + SH + W // 2], strip[:, 0])
                    put(rows[:, :, 1 + SH + W // 2:1 + W - SH], strip[:, 1, 0:NP - 1])
                    put(rows[:, :, 1 + W - SH:1 + W], strip[:, 1, NP - 1:NP, :, 0:SH])
                    put(rows[:, :, 1:1 + SH], strip[:, 1, NP - 1:NP, :, SH:WS])

            def sums(b, jj, k):
                u = b * NT + 2 * jj + k
                total = tap_out[:, TAP_ORDER[2], :, :]
                pool.wait_ge(tap_done, FREE + 4 * u + 3)
                nc.gpsimd.tensor_tensor(total, total, tap_out[:, TAP_ORDER[0], :, :], ALU.add).then_inc(sum_done, 1)
                pool.wait_ge(sum_done, 2 * u + 3)
                nc.gpsimd.tensor_tensor(total, total, tap_out[:, TAP_ORDER[1], :, :], ALU.add).then_inc(sum_done, 1)
                pool.wait_ge(sum_done, 2 * u + 4)
                pool.wait_ge(tap_done, FREE + 4 * u + 4)
                pool.wait_ge(stored[k], FREE + 16 * (b * (NS // 2) + jj))
                nc.gpsimd.tensor_tensor(oo[:, k, :, :], total, tap_out[:, TAP_ORDER[3], :, :], ALU.add).then_inc(oo_done, 1)

            to_image(0, 0)
            with pool.Fori(0, B) as b:
                with pool.Fori(1, NS) as i:
                    to_image(b, i)
                with pool.Fori(0, EARLY) as jj:
                    for k in range(2):
                        sums(b, jj, k)
                to_image(b + 1, 0)
                with pool.Fori(EARLY, NS // 2 - 1) as jj:
                    for k in range(2):
                        sums(b, jj, k)
                sums(b, NS // 2 - 1, 0)

        @block.tensor
        def _(pe):
            mm = nc.tensor.matmul

            def d_of(s, c):
                pe.wait_ge(x_loaded[c], 16 * (s + 1))
                if not isinstance(s, int):
                    pe.wait_ge(xn_done, 4 * s + 2 * c)
                elif s > 0:
                    pe.wait_ge(xn_done, 4 * (s - 1) + 2 * (c + 1))
                mm(d_bank(s, c), center[:], xc[:, c, :], start=True, stop=True).then_inc(d_done, 1)

            def var_of(s, c):
                pe.wait_ge(sq_done, 2 * s + c + 1)
                mm(ps_var, mean_w[:], sq[:], start=True, stop=True).then_inc(var_done, 1)

            pe.wait_ge(ln_loaded, 16)
            d_of(0, 0)
            d_of(0, 1)
            var_of(0, 0)
            pe.wait_ge(w_loaded, 16 * W_LOADS)
            mm(banks_s[:QK, 0, 0:1], wqk[:], ln_b[:], start=True, stop=True).then_inc(pe_set, 1)
            mm(banks_s[:C, 0, 1:2], wvs[:], ln_b[:], start=True, stop=True).then_inc(pe_set, 1)
            var_of(0, 1)
            d_of(1, 0)

            def windows(w):
                return xn[:, :, SH + w * W // 2:SH + (w + 1) * W // 2].rearrange("c r (p x) -> c p r x", x=WS)

            def vs_of(s):
                pe.wait_ge(xn_done, 4 * (s + 1))
                if not (isinstance(s, int) and s == 0):
                    pe.wait_ge(kd_done, 6 * s)
                    pe.wait_ge(kd_dve_done, 2 * s)
                    pe.wait_ge(qd_done, 2 * s)
                for w in range(2):
                    mm(banks_g[:C, w, :], wvs[:], windows(w), start=True, stop=True).then_inc(vs_done, 1)

            def keys_queries(s):
                for w in range(2):
                    pe.wait_ge(vw_done, 2 * s + w + 1)
                    mm(banks_g[:QK, w, :], wqk[:], windows(w), start=True, stop=True).then_inc(kq_done, 1)

            def v_transposed():
                for p in range(NP):
                    last = nc.tensor.transpose(ps_tp[:, p * A:(p + 1) * A],
                                               vw[0:A, p, :, :].rearrange("c w k -> c (w k)"), ident[0:A, 0:A])
                last.then_inc(vt_done, 1)

            pe.wait_ge(dve_set, N_DVE_SET)
            pe.wait_ge(padded, N_PAD)
            vs_of(0)
            d_of(1, 1)
            var_of(1, 0)
            keys_queries(0)
            v_transposed()
            var_of(1, 1)
            pe.wait_ge(xn_done, 8)

            def phase_a(b, i, k):
                t = b * NS + i

                def scores(q):
                    for e in range(2):
                        p = 2 * q + e
                        last = mm(banks_s[:, q % 2, e * 256:(e + 1) * 256],
                                  qd[:, p, :, :].rearrange("c w k -> c (w k)"),
                                  kd[:, p, :, :].rearrange("c h k -> c (h k)"), start=True, stop=True)
                    last.then_inc(s_done, 1)

                def transposes(q):
                    pe.wait_ge(pr_done, FREE + 4 * t + q + 1)
                    if q == 0:
                        pe.wait_ge(vd_done, 4 * (t + 1))
                    else:
                        pe.wait_ge(pt_done, 4 * t + q)
                    for j in range(4):
                        last = nc.tensor.transpose(ps_tp[:, j * 128:(j + 1) * 128],
                                                   pr[:, q % 2, j * 128:(j + 1) * 128], ident[:])
                    last.then_inc(tp_done, 1)

                def values(q):
                    pe.wait_ge(pt_done, 4 * t + q + 1)
                    bank = ps_o if q < 2 else banks_s[:, 1, :]
                    for j in range(4):
                        at = (q % 2) * 208 + j * 52
                        last = mm(bank[:, at:at + 52], pt[:, q, j * 128:(j + 1) * 128],
                                  vd[:, k, 2 * q + j // 2, j % 2, :, :, :].rearrange("k w h d -> k (w h d)"),
                                  start=True, stop=True)
                    last.then_inc(pv_done, 1)

                pe.wait_ge(kd_done, 6 * (t + 1))
                pe.wait_ge(kd_dve_done, 2 * (t + 1))
                pe.wait_ge(qd_done, 2 * (t + 1))
                scores(0)
                scores(1)
                pe.wait_ge(zs_done, FREE + NS * b)
                vs_of(t + 1)
                d_of(t + 2, 0)
                transposes(0)
                pe.wait_ge(sd_done, 4 * t + 1)
                scores(2)
                pe.wait_ge(sd_done, 4 * t + 2)
                scores(3)
                transposes(1)
                var_of(t + 2, 0)
                keys_queries(t + 1)
                transposes(2)
                pe.wait_ge(y1_done, FREE + 2 * t)
                values(0)
                values(1)
                transposes(3)
                pe.wait_ge(sd_done, 4 * (t + 1))
                d_of(t + 2, 1)
                values(2)
                values(3)
                v_transposed()
                var_of(t + 2, 1)
                pe.wait_ge(yq_done, 4 * (t + 1))
                for e in range(4):
                    last = nc.tensor.transpose(ps_o[:C, e * 128:(e + 1) * 128],
                                               yq[:, e, :, :].rearrange("q g c -> q (g c)"), ident[:])
                last.then_inc(yt_done, 1)

            def gate(b):
                pe.wait_ge(kd_done, 6 * (NS * (b + 1) + 1))
                pe.wait_ge(kd_dve_done, 2 * (NS * (b + 1) + 1))
                pe.wait_ge(qd_done, 2 * (NS * (b + 1) + 1))
                one_column(b, fold[:], st[:, 0:1], 0, C, 1)
                one_column(b, fu1T[:], st[:, 5:6], 1, R, 2)
                one_column(b, fu2T[:], tr[:, 1:2], 2, C, 3)

            def one_column(b, lhs, rhs, at, m, dve):
                pe.wait_ge(mid_to_pe, MID_STEPS * b + dve)
                mm(one[0:m, at:at + 1], lhs, rhs, start=True, stop=True).then_inc(mid_pe, 1)

            def projected_means(b):
                one_column(b, spread[:], st[:, 9:10], 3, C, 4)
                one_column(b, projT[:], st[:, 12:13], 4, C, 5)
                one_column(b, projT[:], st[:, 13:14], 5, C, 5)

            def filters(b):
                pe.wait_ge(mid_to_pe, MID_STEPS * b + 7)
                for k in range(4):
                    last = mm(one[0:C, 8 + k:9 + k], w2T[:, k, :], tr[:, 5:6], start=True, stop=True)
                last.then_inc(mid_pe, 1)

            def bank_of(k, c):
                return (banks_g if k == 0 else banks_h)[:C, c, :]

            def project(b, j, k):
                if not (isinstance(j, int) and j < 2):
                    pe.wait_ge(zs_done, FREE + b * NS + j - 1)
                for c in range(2):
                    z = bank_of(k, c)
                    for n, tap in enumerate(PE_TAPS[c]):
                        dh, dw = TAPS[tap]
                        mm(z, proj_t[:, n, :], vsp[:, bass.ds(j * WS + 4 * c + 1 + dh, 4), 1 + dw:1 + dw + W],
                           start=n == 0, stop=False)
                    rows = y1[:, bass.ds((j * WS + H - SH) % H if c == 0 else j * WS, 4), :, :]
                    zh = chunk(z).rearrange("c r (w x) -> c r w x", w=2)
                    half, rest = W // 4, W // 4 - SH
                    mm(zh[:, :, :, SH:SH + half], proj_yc[:, 0, :], rows, start=False, stop=False)
                    mm(zh[:, :, :, SH + half:], proj_yc[:, 1, :], rows[:, :, :, 0:rest], start=False, stop=False)
                    for w in range(2):
                        mm(zh[:, :, 1 - w, 0:SH], proj_yc[:, 1, :], rows[:, :, w, rest:], start=False, stop=False)

            def project_mixed(b, j, k):
                pe.wait_ge(m_step, len(MIX) * (b * NS + j + 1))
                for c in range(2):
                    last = mm(bank_of(k, c), proj_m[:], mb[:, k, 4 * c:4 * c + 4, :], start=False, stop=True)
                last.then_inc(z_done, 1)

            with pe.Fori(0, B) as b:
                with pe.Fori(0, NS // 2) as ii:
                    for k in range(2):
                        phase_a(b, 2 * ii + k, k)
                gate(b)
                projected_means(b)
                one_column(b, w1T[:], st[:, 14:15], 6, R, 6)
                project(b, 0, 0)
                filters(b)
                project_mixed(b, 0, 0)
                pe.wait_ge(vd_done, 4 * (NS * (b + 1) + 1))
                project(b, 1, 1)
                with pe.Fori(0, NS // 2 - 1) as jj:
                    project_mixed(b, 2 * jj + 1, 1)
                    project(b, 2 * jj + 2, 0)
                    project_mixed(b, 2 * jj + 2, 0)
                    project(b, 2 * jj + 3, 1)
                project_mixed(b, NS - 1, 1)

        @block.scalar
        def _(act):
            for s in (pr_done, y1_done, tap_done):
                act.sem_inc(s, FREE)
            fn = nc.scalar.activation
            act.preload_act_table_set("natural_log_exp_and_others")

            def square(s, c):
                act.wait_ge(d_done, 2 * s + c + 1)
                fn(sq[:], d_bank(s, c), ACT.Square).then_inc(sq_done, 1)

            def rsqrt(s, c):
                act.wait_ge(var_done, 2 * s + c + 1)
                fn(lnv[:], ps_var, ACT.Ln, bias=eps[:, 0:1]).then_inc(ln_done, 1)
                act.wait_ge(ln_done, 2 * s + c + 1)
                if isinstance(s, int) and 2 * s + c > 0:
                    act.wait_ge(xn_done, 2 * (2 * s + c))
                fn(rstd[:], lnv[:], ACT.Exp, scale=-0.5).then_inc(rstd_done, 1)

            act.wait_ge(eps_set, 2)
            for c in range(2):
                square(0, c)
                rsqrt(0, c)
            act.wait_ge(w_loaded, 16 * W_LOADS)
            fn(bn_scale[:], bn[:, 3:4], ACT.Ln, bias=eps[:R, 1:2]).then_inc(act_set, 1)
            act.wait_ge(act_set, 1)
            fn(bn_scale[:], bn_scale[:], ACT.Exp, scale=-0.5).then_inc(act_set, 1)
            act.wait_ge(dve_set, N_DVE_SET)
            act.wait_ge(padded, N_PAD)

            def keys(s, w, heads):
                act.wait_ge(kq_done, 2 * s + w + 1)
                if w == 1:
                    act.wait_ge(kd_dve_done, 2 * (s + 1))
                r = slice(SECOND, QK)
                for h in heads:
                    fn(kd[w * SECOND:w * SECOND + A, :, h, :], banks_g[r, w, :].rearrange("c (p k) -> c p k", k=K),
                       ACT.Identity, bias=k_bias[r, h:h + 1], scale=head_mask[r, h:h + 1]).then_inc(kd_done, 1)

            def vs_out(s, w):
                act.wait_ge(vs_done, 2 * s + w + 1)
                if not (isinstance(s, int) and s == 0) and w == 0:
                    act.wait_ge(vsp_done, 8 * s)
                fn(vw[:, :, w, :], banks_g[:C, w, :].rearrange("c (p k) -> c p k", k=K), ACT.Identity,
                   bias=vs_bias[:], accum_out=vstat[:, bass.ds(2 * s + w, 1)]).then_inc(vw_done, 1)

            def values(s, k):
                act.wait_ge(vt_done, s + 1)
                for wi in range(2):
                    for h in range(2):
                        src = ps_tp[wi * K:(wi + 1) * K, 0:NP * A].rearrange(
                            "k (p s h d) -> k p s h d", s=2, h=2, d=HD)
                        fn(vd[h * K:(h + 1) * K, k, :, :, wi, h, 0:HD], src[:, :, :, h, :], ACT.Copy).then_inc(vd_done, 1)

            square(1, 0)
            vs_out(0, 0)
            vs_out(0, 1)
            rsqrt(1, 0)
            square(1, 1)
            keys(0, 0, (0, 1, 2, 3))
            keys(0, 1, (0, 1))
            rsqrt(1, 1)
            values(0, 0)

            def phase_a(b, i, k):
                t = b * NS + i

                def exps(q):
                    act.wait_ge(sd_done, 4 * t + q + 1)
                    fn(pr[:, q % 2, :], sd[:, q % 2, :], ACT.Exp).then_inc(pr_done, 1)

                def transposed(q):
                    act.wait_ge(tp_done, 4 * t + q + 1)
                    fn(pt[:, q, :], ps_tp[:, :], ACT.Copy).then_inc(pt_done, 1)

                exps(0)
                vs_out(t + 1, 0)
                transposed(0)
                exps(1)
                square(t + 2, 0)
                vs_out(t + 1, 1)
                transposed(1)
                exps(2)
                rsqrt(t + 2, 0)
                exps(3)
                transposed(2)
                keys(t + 1, 0, (0, 1))
                transposed(3)
                keys(t + 1, 0, (2, 3))
                square(t + 2, 1)
                keys(t + 1, 1, (0, 1))
                rsqrt(t + 2, 1)
                act.wait_ge(yt_done, t + 1)
                src = ps_o[:C, :].rearrange("c (e w r x) -> c e w r x", e=4, w=2, x=WS)
                for wi in range(2):
                    dst = y1[:, bass.ds(i * WS, WS), wi, :].rearrange("c r (e x) -> c e r x", x=WS)
                    fn(dst, src[:, :, wi, :, :], ACT.Copy,
                       accum_out=ystat[:, bass.ds(2 * i + wi, 1)]).then_inc(y1_done, 1)
                values(t + 1, 1 - k)

            def first(b, j, k):
                if isinstance(j, int):
                    act.wait_ge(vsp_done, 8 * NS * (b + 1))
                else:
                    act.wait_ge(z_done, b * NS + j - 1)
                dh, dw = TAPS[ACT_TAP]
                for c in (1, 0):
                    fn(mb[:, k, 4 * c:4 * c + 4, :], vsp[:, bass.ds(j * WS + 4 * c + 1 + dh, 4), 1 + dw:1 + dw + W],
                       ACT.Copy, scale=depth_w[:, ACT_TAP:ACT_TAP + 1]).then_inc(first_done, 1)

            def taps(b, j, k):
                u = b * NT + j
                act.wait_ge(zs_done, FREE + b * NS + j + 1)
                fn(zs[:, k, 0, :], zs[:, 1 - k, WS, :], ACT.Copy).then_inc(halo_done, 1)
                act.wait_ge(halo_done, u + 1)
                for n, tap in enumerate(TAP_ORDER):
                    if n < 2:
                        act.wait_ge(sum_done, 2 * u + n + 1)
                    elif n == 2:
                        act.wait_ge(oo_done, FREE + u)
                    dh, dw = L1_TAPS[tap]
                    fn(tap_out[:, tap, :, :], zs[:, k, 1 + dh:1 + dh + WS, 1 + dw:1 + dw + W],
                       ACT.Identity, scale=l1_w[:, tap:tap + 1],
                       bias=l1_b[:] if tap == 0 else 0.0).then_inc(tap_done, 1)

            with act.Fori(0, B) as b:
                with act.Fori(0, NS // 2) as ii:
                    for k in range(2):
                        phase_a(b, 2 * ii + k, k)
                first(b, 0, 0)
                first(b, 1, 1)
                act.wait_ge(mid_pe, MID_PE * b + 3)
                fn(st[:, 6:7], one[:C, 2:3], ACT.Exp, scale=-1.0).then_inc(mid_act, 1)
                with act.Fori(0, NS // 2 - 1) as jj:
                    for k in range(2):
                        first(b, 2 * jj + 2 + k, k)
                        taps(b, 2 * jj + k, k)
                taps(b, NS - 2, 0)

        @block.vector
        def _(dve):
            dve.sem_inc(zs_done, FREE)
            v = nc.vector

            def sum_x(s, c):
                dve.wait_ge(x_loaded[c], 16 * (s + 1))
                v.tensor_reduce(xstat[:, bass.ds(2 * s + c, 1)], xc[:, c, :], AX.X, ALU.add).then_inc(xsum_done, 1)

            def normalise(s, c):
                dve.wait_ge(rstd_done, 2 * s + c + 1)
                d, r = chunk(d_bank(s, c)), chunk(rstd[:])
                rows = xn[:, 4 * c:4 * c + 4, :]
                if not (isinstance(s, int) and s == 0):
                    dve.wait_ge(kq_done, 2 * s)
                v.tensor_tensor(rows[:, :, 0:W], d, r, ALU.mult).then_inc(xn_done, 1)
                v.tensor_tensor(rows[:, :, W:XW], d[:, :, 0:SH], r[:, :, 0:SH], ALU.mult).then_inc(xn_done, 1)

            def queries(s):
                for w in range(2):
                    dve.wait_ge(kq_done, 2 * s + w + 1)
                    bank = banks_g[:, w, :].rearrange("c (p k) -> c p k", k=K)
                    dst = slice(w * SECOND, w * SECOND + A)
                    v.tensor_scalar(qd[dst, :, w, :], bank[0:A], qk_b[0:A, :], SCALE, ALU.add, ALU.mult).then_inc(qd_done, 1)

            def keys(s):
                r = slice(SECOND, QK)
                for h in (2, 3):
                    v.tensor_scalar(kd[SECOND:QK, :, h, :], banks_g[r, 1, :].rearrange("c (p k) -> c p k", k=K),
                                    head_mask[r, h:h + 1], k_bias[r, h:h + 1], ALU.mult, ALU.add).then_inc(kd_dve_done, 1)

            for c in range(2):
                sum_x(0, c)
            for c in range(2):
                normalise(0, c)
            dve.wait_ge(pe_set, 2)
            n = [0]

            def setup(ins):
                ins.then_inc(dve_set, 1)
                n[0] += 1
                dve.wait_ge(dve_set, n[0])

            dve.wait_ge(w_loaded, 16 * W_LOADS)
            for t in (wqk, wvs):
                setup(v.tensor_scalar(t[:], t[:], ln_w[:], None, ALU.mult))
            setup(v.tensor_tensor(qk_b[:], banks_s[:QK, 0, 0:1], qk_b[:], ALU.add))
            setup(v.tensor_tensor(vs_bias[:], banks_s[:C, 0, 1:2], vs_b[:], ALU.add))
            setup(v.tensor_scalar(k_bias[:], head_mask[:], qk_b[:], None, ALU.mult))
            dve.wait_ge(act_set, 2)
            setup(v.tensor_tensor(bn_scale[:], bn_scale[:], bn[:, 0:1], ALU.mult))
            assert n[0] == N_DVE_SET

            dve.wait_ge(padded, N_PAD)
            for c in range(2):
                sum_x(1, c)
            queries(0)
            keys(0)
            for c in range(2):
                normalise(1, c)

            def phase_a(b, i, last=False):
                t = b * NS + i

                def softmax(q):
                    dve.wait_ge(s_done, 4 * t + q + 1)
                    s = banks_s[:, q % 2, :].rearrange("p (g k) -> p g k", k=K)
                    v.tensor_reduce(mx[:, q, :], s, AX.X, ALU.max).then_inc(mx_done, 1)
                    dve.wait_ge(mx_done, 4 * t + q + 1)
                    if q < 2:
                        dve.wait_ge(pr_done, FREE + 4 * t)
                    else:
                        dve.wait_ge(pr_done, FREE + 4 * t + q - 1)
                    v.tensor_tensor(sd[:, q % 2, :].rearrange("p (g k) -> p g k", k=K), s,
                                    mx[:, q, :].unsqueeze(2).to_broadcast([128, 8, K]),
                                    ALU.subtract).then_inc(sd_done, 1)

                def divide(half):
                    dve.wait_ge(pv_done, 4 * t + 2 * half + 2)
                    bank = ps_o if half == 0 else banks_s[:, 1, :]
                    o = bank[:, 0:416].rearrange("q (n w h d) -> q n w h d", w=2, h=2, d=VW)
                    for wi in range(2):
                        r = slice(wi * K, (wi + 1) * K)
                        rc = rec[r, half, :].rearrange("q (n h) -> q n h", h=2)
                        v.reciprocal(rc, o[r, :, wi, :, HD]).then_inc(rec_done, 1)
                    for wi in range(2):
                        dve.wait_ge(rec_done, 4 * t + 2 * half + wi + 1)
                        r = slice(wi * K, (wi + 1) * K)
                        rc = rec[r, half, :].rearrange("q (n h) -> q n h", h=2)
                        v.tensor_tensor(yq[r, :, half, :].rearrange("q e (s h d) -> q e s h d", s=2, d=HD),
                                        o[r, :, wi, :, 0:HD].rearrange("q (e s) h d -> q e s h d", s=2), rc.rearrange("q (e s) h -> q e s h", s=2).unsqueeze(4).to_broadcast([K, 4, 2, 2, HD]),
                                        ALU.mult).then_inc(yq_done, 1)

                softmax(0)
                softmax(1)
                sum_x(t + 2, 0)
                softmax(2)
                softmax(3)
                sum_x(t + 2, 1)
                queries(t + 1)
                normalise(t + 2, 0)
                divide(0)
                keys(t + 1)
                if last:
                    image_sums(b)
                divide(1)
                if last:
                    local_mean(b)
                normalise(t + 2, 1)

            n, k = [0], [0]
            s = lambda i, w=1: st[:, i:i + w]

            def step(ins):
                ins.then_inc(mid_dve, 1)
                n[0] += 1

            def settle(b):
                dve.wait_ge(mid_dve, N_MID * b + n[0])

            def to_pe(b, ins):
                ins.then_inc(mid_to_pe, 1)
                k[0] += 1
                dve.wait_ge(mid_to_pe, MID_STEPS * b + k[0])

            def image_sums(b):
                img = vsp[:, 1:1 + H, 1:1 + W]
                dve.wait_ge(vsp_done, 8 * NS * (b + 1))
                dve.wait_ge(xsum_done, 2 * NS * (b + 1))
                step(v.tensor_reduce(s(1), vstat[:, bass.ds(2 * NS * b, 2 * NS)], AX.X, ALU.add))
                step(v.tensor_reduce(s(2), xstat[:, bass.ds(2 * NS * b, 2 * NS)], AX.X, ALU.add))
                for at, rows in ((0, H - 1), (2, 0)):
                    step(v.tensor_reduce(edge[:, at:at + 1], img[:, rows, :], AX.X, ALU.add))
                    step(v.tensor_reduce(edge[:, 3 + at:4 + at], img[:, :, rows], AX.X, ALU.add))
                    for bt, cols in ((0, W - 1), (2, 0)):
                        step(v.tensor_copy(edge[:, 6 + 3 * at + bt:7 + 3 * at + bt], img[:, rows, cols:cols + 1]))

            def local_mean(b):
                e3 = edge[:, 6:15].rearrange("c (a b) -> c a b", b=3)
                sums = edge[:, 15:24].rearrange("c (a b) -> c a b", b=3)
                settle(b)
                step(v.tensor_tensor(sums, e3, edge[:, 0:3].unsqueeze(2).to_broadcast([C, 3, 3]), ALU.subtract))
                step(v.tensor_tensor(s(8), s(1), upper, ALU.mult))
                settle(b)
                step(v.tensor_tensor(sums, sums, edge[:, 3:6].unsqueeze(1).to_broadcast([C, 3, 3]), ALU.subtract))
                settle(b)
                step(v.tensor_scalar(edge[:, 15:24], edge[:, 15:24], s(1), 1.0 / PX, ALU.add, ALU.mult))
                settle(b)
                step(v.tensor_tensor(edge[:, 15:24], edge[:, 15:24], depth_w, ALU.mult))
                settle(b)
                step(v.tensor_reduce(s(3), edge[:, 15:24], AX.X, ALU.add))
                settle(b)
                step(v.tensor_tensor(s(3), s(3), depth_b, ALU.add))
                dve.wait_ge(tap_done, FREE + 4 * NT * b)
                step(v.memset(zs[:, 1, WS, :], 0.0))
                settle(b)

            def mean_y(b):
                dve.wait_ge(y1_done, FREE + 2 * NS * (b + 1))
                to_pe(b, v.tensor_reduce(s(0), ystat[:], AX.X, ALU.add))

            def squeeze_in(b):
                dve.wait_ge(mid_pe, MID_PE * b + 1)
                step(v.tensor_scalar(s(4), one[:C, 0:1], s(8), 1.0 / PX, ALU.add, ALU.mult))
                settle(b)
                to_pe(b, v.tensor_tensor(s(5), s(4), s(3), ALU.add))

            def leaky(b):
                dve.wait_ge(mid_pe, MID_PE * b + 2)
                step(v.tensor_scalar(tr[:, 0:1], one[:R, 1:2], 0.2, None, ALU.mult))
                settle(b)
                to_pe(b, v.tensor_tensor(tr[:, 1:2], one[:R, 1:2], tr[:, 0:1], ALU.max))

            def gate(b):
                dve.wait_ge(mid_act, b + 1)
                step(v.tensor_scalar(s(7), s(6), 1.0, None, ALU.add))
                settle(b)
                to_pe(b, v.reciprocal(s(9), s(7)))
                step(v.tensor_scalar(s(10), s(9), -1.0, 1.0, ALU.mult, ALU.add))
                settle(b)
                step(v.tensor_tensor(s(16), s(9), upper, ALU.mult))
                step(v.tensor_scalar(tap_w[:], depth_w, s(10), None, ALU.mult))
                step(v.tensor_tensor(s(11), s(4), s(9), ALU.mult))
                step(v.tensor_tensor(s(13), depth_b, s(10), ALU.mult))
                settle(b)
                step(v.tensor_tensor(tap_w[:, 4:5], tap_w[:, 4:5], s(16), ALU.add))
                to_pe(b, v.scalar_tensor_tensor(out=s(12), in0=s(3), scalar=s(10), in1=s(11), op0=ALU.mult, op1=ALU.add))

            def projections(b):
                settle(b)
                step(v.tensor_scalar(proj_m[:], projT, s(10), None, ALU.mult))
                for m, tap in enumerate(PE_TAPS[0]):
                    step(v.tensor_scalar(proj_t[:, m, :], projT, tap_w[:, tap:tap + 1], None, ALU.mult))

            def pooled(b):
                dve.wait_ge(mid_pe, MID_PE * b + 6)
                step(v.tensor_tensor(s(15), one[:C, 4:5], proj_b, ALU.add))
                step(v.tensor_copy(s(17), one[:C, 3:4]))
                step(v.tensor_tensor(z_bias[:], one[:C, 5:6], proj_b, ALU.add))
                settle(b)
                step(v.tensor_scalar(proj_yc[:].rearrange("c g o -> c (g o)"), proj_y, s(17), None, ALU.mult))
                settle(b)
                to_pe(b, v.scalar_tensor_tensor(out=s(14), in0=s(2), scalar=1.0 / PX, in1=s(15), op0=ALU.mult, op1=ALU.add))

            def squeeze(b):
                dve.wait_ge(mid_pe, MID_PE * b + 7)
                step(v.tensor_tensor(tr[:, 3:4], one[:R, 6:7], bn[:, 2:3], ALU.subtract))
                settle(b)
                step(v.scalar_tensor_tensor(out=tr[:, 4:5], in0=tr[:, 3:4], scalar=bn_scale[:], in1=bn[:, 1:2],
                                            op0=ALU.mult, op1=ALU.add))
                settle(b)
                to_pe(b, v.tensor_scalar(tr[:, 5:6], tr[:, 4:5], 0.0, None, ALU.max))

            def filters(b):
                dve.wait_ge(mid_pe, MID_PE * (b + 1))
                to_pe(b, v.tensor_tensor(l1_w[:], one[:C, 8:12], b2, ALU.add))
                assert (n[0], k[0]) == (N_MID, MID_STEPS), (n, k)

            def mix(b, j, k, steps=range(len(MIX))):
                u = b * NS + j
                for m in steps:
                    c, tap = MIX[m]
                    if m < 2:
                        dve.wait_ge(first_done, 2 * u + m + 1)
                    else:
                        dve.wait_ge(m_step, len(MIX) * u + m - 1)
                    dh, dw = TAPS[tap]
                    acc = mb[:, k, 4 * c:4 * c + 4, :]
                    v.scalar_tensor_tensor(out=acc, in0=vsp[:, bass.ds(j * WS + 4 * c + 1 + dh, 4), 1 + dw:1 + dw + W],
                                           scalar=depth_w[:, tap:tap + 1], in1=acc,
                                           op0=ALU.mult, op1=ALU.add).then_inc(m_step, 1)

            def finish(b, j, jj, k):
                u = b * NS + j
                dve.wait_ge(z_done, u + 1)
                dve.wait_ge(x0_loaded[k], 16 * (b * (NS // 2) + jj + 1))
                if isinstance(j, int) and j == 0:
                    dve.wait_ge(tap_done, FREE + 4 * NT * b)
                else:
                    dve.wait_ge(tap_done, FREE + 4 * (b * NT + j - 1))
                    dve.wait_ge(halo_done, b * NT + j)
                z = (banks_g if k == 0 else banks_h)[:C, :, :].rearrange("c a (r x) -> c (a r) x", x=W)
                v.scalar_tensor_tensor(out=zs[:, k, 1:1 + WS, 1:1 + W], in0=z, scalar=z_bias[:],
                                       in1=x0[:, k, :, :], op0=ALU.add, op1=ALU.add).then_inc(zs_done, 1)

            def last_strip(b):
                def step(ins):
                    ins.then_inc(last_step, 1)

                dve.wait_ge(zs_done, FREE + NS * (b + 1))
                step(v.tensor_copy(zs[:, 1, 0, :], zs[:, 0, WS, :]))
                for tap in range(len(L1_TAPS)):
                    dh, dw = L1_TAPS[tap]
                    for c in (1, 0):
                        rows = slice(4 * c, 4 * c + 4)
                        src = zs[:, 1, 1 + dh + 4 * c:5 + dh + 4 * c, 1 + dw:1 + dw + W]
                        if tap == 0:
                            if c == 0:
                                dve.wait_ge(last_step, LAST_STEPS * b + 1)
                            step(v.tensor_scalar(x0[:, 1, rows, :], src, l1_w[:, 0:1], l1_b[:], ALU.mult, ALU.add))
                        else:
                            dve.wait_ge(last_step, LAST_STEPS * b + 1 + 2 * tap - 1 + (1 - c))
                            step(v.scalar_tensor_tensor(out=x0[:, 1, rows, :], in0=src, scalar=l1_w[:, tap:tap + 1],
                                                        in1=x0[:, 1, rows, :], op0=ALU.mult, op1=ALU.add))

            with dve.Fori(0, B) as b:
                with dve.Fori(0, NS - 1) as i:
                    phase_a(b, i)
                phase_a(b, NS - 1, last=True)
                mean_y(b)
                for at, part in enumerate((squeeze_in, leaky, gate, projections, pooled, squeeze)):
                    mix(b, 0, 0, FILL[at])
                    part(b)
                mix(b, 0, 0, FILL[-1])
                mix(b, 1, 1)
                filters(b)
                finish(b, 0, 0, 0)
                with dve.Fori(0, NS // 2 - 1) as jj:
                    mix(b, 2 * jj + 2, 0)
                    finish(b, 2 * jj + 1, jj, 1)
                    mix(b, 2 * jj + 3, 1)
                    finish(b, 2 * jj + 2, jj + 1, 0)
                finish(b, NS - 1, NS // 2 - 1, 1)
                last_strip(b)


def kernel(**inputs):
    import concourse.bacc as bacc
    from concourse.bass_utils import run_bass_kernel_spmd

    arr = {k: np.asarray(v) for k, v in inputs.items()}
    l0 = {k[len("L0_conv_"):]: v for k, v in arr.items() if k.startswith("L0_conv_")}
    l1 = {k[len("L1_conv_"):]: v for k, v in arr.items() if k.startswith("L1_conv_")}
    col = lambda a: a.reshape(-1, 1)
    row = np.arange(C)
    w = {
        "center": np.eye(C) - 1.0 / C,
        "mean_w": np.full((C, C), 1.0 / C),
        "ident": np.eye(128),
        "fold": row[:, None] % A == row[None, :],
        "spread": row[:, None] == row[None, :] % A,
        "head_mask": (np.arange(QK)[:, None] % SECOND) // HD == np.arange(HEADS)[None, :],
        "upper": row[:, None] >= A,
    }
    w = {k: v.astype(np.float32) for k, v in w.items()}
    w |= {"qkT": l0["qk_w"].T, "qk_b": col(l0["qk_b"])}
    wqk, qk_b = np.zeros((C, QK), np.float32), np.zeros((QK, 1), np.float32)
    wqk[:, 0:A], wqk[:, SECOND:QK] = w["qkT"][:, 0:A], w["qkT"][:, A:2 * A]
    qk_b[0:A], qk_b[SECOND:QK] = w["qk_b"][0:A], w["qk_b"][A:2 * A]
    proj_y = np.zeros((C, 2, C), np.float32)
    proj_y[0:A, 0], proj_y[A:C, 1] = l0["proj_w"].T[0:A], l0["proj_w"].T[0:A]
    w |= {
        "wqk": wqk, "qk_b": qk_b, "proj_y": proj_y.reshape(C, 2 * C),
        "wvs": l0["vs_w"].T, "projT": l0["proj_w"].T,
        "fu1T": l0["fu1_w"].T, "fu2T": l0["fu2_w"].T, "w1T": l1["w1"].T,
        "w2T": l1["w2"].reshape(C, 9, R)[:, 0:4].transpose(2, 1, 0).reshape(R, 4 * C),
        "ln_w": col(l0["ln_w"]), "ln_b": col(l0["ln_b"]), "vs_b": col(l0["vs_b"]),
        "depth_w": l0["depth_w"].reshape(C, 9), "depth_b": col(l0["depth_b"]), "proj_b": col(l0["proj_b"]),
        "bn": np.stack([l1["gamma"], l1["beta"], l1["running_mean"], l1["running_var"]], 1),
        "b2": l1["b2"].reshape(C, 9)[:, 0:4], "l1_b": col(l1["bias"]),
    }
    w = {"ident": w["ident"]} | {name: np.concatenate([w[what] for what, _ in columns], 1)
                                 for name, (_, columns) in PACKS.items()}
    arrays = {"in_x": arr["x"].reshape(B, C, H, W)} | {f"in_{k}": v for k, v in w.items()}
    arrays = {k: np.ascontiguousarray(v) for k, v in arrays.items()}

    nc = bacc.Bacc("TRN2", target_bir_lowering=False, num_devices=1)
    dram = {k: nc.dram_tensor(k, v.shape, F32, kind="ExternalInput").ap() for k, v in arrays.items()}
    out = nc.dram_tensor("out_0", (B, C, H, W), F32, kind="ExternalOutput").ap()
    program(nc, dram["in_x"], out, {k[3:]: v for k, v in dram.items()})
    return run_bass_kernel_spmd(nc, [arrays], core_ids=[0]).results[0]["out_0"]
```
